# Optimizing a Trainium2 kernel written in Bass

```python
import numpy as np
import jax
import jax.numpy as jnp

def _softmax(x, axis=-1):
    return jax.nn.softmax(x, axis=axis)

def _gelu(x):
    return jax.nn.gelu(x, approximate=True)

def _silu(x):
    return jax.nn.silu(x)

def _sigmoid(x):
    return jax.nn.sigmoid(x)

def _layernorm(x, axis=-1, eps=1e-05):
    m = jnp.mean(x, axis=axis, keepdims=True)
    v = jnp.var(x, axis=axis, keepdims=True)
    return (x - m) / jnp.sqrt(v + eps)

def _scatter_add(tgt, idx, src, axis=0):
    return tgt.at[idx].add(src)

def _segment_sum(src, seg, n):
    return jax.ops.segment_sum(src, seg, n)
kernel_name = 'mk_adaln_d1_jaxref_r4_8c4886'

def setup_inputs(seed: int=0):
    np.random.seed(seed)
    _w = jnp.asarray

    def _L0_attn_setup():
        import jax, jax.numpy as jnp
        import numpy as np
        B, S, D = (4, 512, 256)
        key = jax.random.key(seed)
        k1, k2 = jax.random.split(key)
        x = jax.random.normal(k1, (B, S, D), dtype=jnp.float32)
        W = jax.random.normal(k2, (2 * D, D), dtype=jnp.float32) * 0.02
        return {'x': x, 'W': W}
    _L0_attn_in = _L0_attn_setup()

    def _L0_ffn_setup():
        import jax, jax.numpy as jnp
        import numpy as np
        H = 256
        I = 128
        E = 32
        TOP_K = 6
        N_GROUP = 8
        TOPK_GROUP = 4
        SCALE = 2.5
        N_SHARED = 2
        SI = I * N_SHARED
        B, S = (2, 256)
        key = jax.random.key(seed)
        ks = jax.random.split(key, 8)
        x = jax.random.normal(ks[0], (B, S, H), jnp.float32)
        gate_weight = jax.random.normal(ks[1], (E, H), jnp.float32) * 0.02
        e_score_correction_bias = jax.random.normal(ks[2], (E,), jnp.float32) * 0.01
        experts_gate_up = jax.random.normal(ks[3], (E, 2 * I, H), jnp.float32) * 0.02
        experts_down = jax.random.normal(ks[4], (E, H, I), jnp.float32) * 0.02
        shared_gate_w = jax.random.normal(ks[5], (SI, H), jnp.float32) * 0.02
        shared_up_w = jax.random.normal(ks[6], (SI, H), jnp.float32) * 0.02
        shared_down_w = jax.random.normal(ks[7], (H, SI), jnp.float32) * 0.02
        return {'x': x, 'gate_weight': gate_weight, 'e_score_correction_bias': e_score_correction_bias, 'experts_gate_up': experts_gate_up, 'experts_down': experts_down, 'shared_gate_w': shared_gate_w, 'shared_up_w': shared_up_w, 'shared_down_w': shared_down_w}
    _L0_ffn_in = _L0_ffn_setup()
    _L0_c = _w((lambda *s: np.random.randn(*s).astype(np.float32) * 0.05)(8, 256))
    _L0_wmod = _w((lambda *s: np.random.randn(*s).astype(np.float32) * 0.05)(256, 6 * 256) * 256 ** (-0.5))
    _d = {'L0_attn_x': _L0_attn_in['x'], 'L0_attn_W': _L0_attn_in['W'], 'L0_ffn_gate_weight': _L0_ffn_in['gate_weight'], 'L0_ffn_e_score_correction_bias': _L0_ffn_in['e_score_correction_bias'], 'L0_ffn_experts_gate_up': _L0_ffn_in['experts_gate_up'], 'L0_ffn_experts_down': _L0_ffn_in['experts_down'], 'L0_ffn_shared_gate_w': _L0_ffn_in['shared_gate_w'], 'L0_ffn_shared_up_w': _L0_ffn_in['shared_up_w'], 'L0_ffn_shared_down_w': _L0_ffn_in['shared_down_w'], 'L0_c': _L0_c, 'L0_wmod': _L0_wmod}
    _x0 = _d['L0_attn_x']
    _d['L0_attn_x'] = jax.random.normal(jax.random.fold_in(jax.random.key(seed), 1), (8, 512, 256), dtype=_x0.dtype)
    del _x0
    return _d

def reference(L0_attn_x, L0_attn_W, L0_ffn_gate_weight, L0_ffn_e_score_correction_bias, L0_ffn_experts_gate_up, L0_ffn_experts_down, L0_ffn_shared_gate_w, L0_ffn_shared_up_w, L0_ffn_shared_down_w, L0_c, L0_wmod):

    def _L0_attn_ref(x, W):
        import jax, jax.numpy as jnp
        import numpy as np
        B, S, D = (4, 512, 256)
        d = x.shape[-1]
        kv = x @ W.T
        K, V = (kv[..., :d], kv[..., d:])
        n = x.shape[-2]
        causal = jnp.tril(jnp.ones((n, n), dtype=bool))
        mask = jnp.where(causal, jnp.float32(0.0), -jnp.inf).astype(x.dtype)
        scores = jnp.einsum('bqd,bkd->bqk', x, K) + mask
        attn = jax.nn.softmax(scores, axis=-1)
        return x + jnp.einsum('bqk,bkd->bqd', attn, V)

    def _L0_ffn_ref(x, gate_weight, e_score_correction_bias, experts_gate_up, experts_down, shared_gate_w, shared_up_w, shared_down_w):
        import jax, jax.numpy as jnp
        import numpy as np
        H = 256
        I = 128
        E = 32
        TOP_K = 6
        N_GROUP = 8
        TOPK_GROUP = 4
        SCALE = 2.5
        N_SHARED = 2
        SI = I * N_SHARED
        B, S = (2, 256)
        b, s, h = x.shape
        xf = x.reshape(-1, h)
        T = xf.shape[0]
        logits = xf.astype(jnp.float32) @ gate_weight.astype(jnp.float32).T
        scores = jax.nn.sigmoid(logits)
        sfc = scores + e_score_correction_bias[None, :]
        gs = E // N_GROUP
        group_scores = sfc.reshape(T, N_GROUP, gs).max(axis=-1)
        _, gidx = jax.lax.top_k(group_scores, TOPK_GROUP)
        gmask = jnp.zeros((T, N_GROUP), bool).at[jnp.arange(T)[:, None], gidx].set(True)
        smask = jnp.repeat(gmask, gs, axis=1)
        masked = jnp.where(smask, sfc, 0.0)
        _, topk_idx = jax.lax.top_k(masked, TOP_K)
        tw = jnp.take_along_axis(scores, topk_idx, axis=1)
        tw = tw / (tw.sum(-1, keepdims=True) + 1e-20)
        tw = (tw * SCALE).astype(xf.dtype)
        combine = jnp.zeros((T, E), xf.dtype).at[jnp.arange(T)[:, None], topk_idx].add(tw)

        def expert_step(acc, inp):
            gu, dn, c = inp
            g = xf @ gu[:I].T
            u = xf @ gu[I:].T
            o = jax.nn.silu(g) * u @ dn.T
            return (acc + c[:, None] * o, None)
        routed, _ = jax.lax.scan(expert_step, jnp.zeros_like(xf), (experts_gate_up, experts_down, combine.T))
        sh = jax.nn.silu(xf @ shared_gate_w.T) * (xf @ shared_up_w.T)
        shared_out = sh @ shared_down_w.T
        return (routed + shared_out).reshape(b, s, h)
    x = L0_attn_x
    mod = (_silu(L0_c) @ L0_wmod).reshape(L0_c.shape[0], 6, 1, -1)
    sa, ca, ga, sb, cb, gb = (mod[:, 0], mod[:, 1], mod[:, 2], mod[:, 3], mod[:, 4], mod[:, 5])
    ga = (2 * (ga >= 0) - 1) * jnp.maximum(jnp.abs(ga), 0.25)
    gb = (2 * (gb >= 0) - 1) * jnp.maximum(jnp.abs(gb), 0.25)
    h = _layernorm(x, axis=-1) * (1 + ca) + sa
    x = x + ga * _L0_attn_ref(h, L0_attn_W)
    h = _layernorm(x, axis=-1) * (1 + cb) + sb
    x = x + gb * _L0_ffn_ref(h, L0_ffn_gate_weight, L0_ffn_e_score_correction_bias, L0_ffn_experts_gate_up, L0_ffn_experts_down, L0_ffn_shared_gate_w, L0_ffn_shared_up_w, L0_ffn_shared_down_w)
    return x

_drawn_inputs = setup_inputs


def setup_inputs(seed=0):
    import zlib

    import numpy as np

    out = dict(_drawn_inputs(seed))
    spreads = {}
    factors = {'L0_ffn_gate_weight': 8.0,
     'L0_ffn_e_score_correction_bias': 8.0,
     'L0_ffn_experts_gate_up': 8.0,
     'L0_ffn_experts_down': 8.0,
     'L0_ffn_shared_gate_w': 8.0,
     'L0_ffn_shared_up_w': 8.0,
     'L0_ffn_shared_down_w': 8.0}
    for name, (base, spread) in spreads.items():
        noise = np.random.default_rng([zlib.crc32(name.encode()), seed]).standard_normal(out[name].shape)
        drawn = base * np.exp(spread * noise) if base else spread * noise
        out[name] = jnp.asarray(drawn.astype(out[name].dtype))
    for name, factor in factors.items():
        out[name] = (out[name] * factor).astype(out[name].dtype)
    return out
```

```python
from contextlib import ExitStack

import concourse.bass as bass
from concourse import mybir

P = 128
ALU = mybir.AluOpType
ACT = mybir.ActivationFunctionType
AX = mybir.AxisListType
F32 = mybir.dt.float32
BF16 = mybir.dt.bfloat16

LN_EPS = 1e-5
MIN_GATE = 0.25
MASKED = -1e30
N_GROUP, TOPK_GROUP, TOP_K, ROUTE_SCALE = 8, 4, 6, 2.5
SENTINEL = -3e38
TAKEN = -2e38
SA, CA, GA, SB, CB, GB = range(6)


def build_adaln_block(nc, x, wT, gateT, bias, guT, dnT, cT, wmod, out):
    B, S, D = x.shape
    E = gateT.shape[1]
    EA = guT.shape[0]
    I = dnT.shape[1]
    KD = D // P
    NT = S // P
    NM = 6 * D
    EG = E // N_GROUP

    with ExitStack() as ctx:
        def sb(name, shape, dt=F32):
            return ctx.enter_context(nc.sbuf_tensor(name, shape, dt))

        def sem(name):
            return ctx.enter_context(nc.semaphore(name))

        xs = sb("xs", [P, B * NT, D])
        h2T = sb("h2T", [P, KD, B * S])
        acc = sb("acc", [P, B * NT, D])
        h2T_s = [sb(f"h2T_s{p}", [P, KD, S]) for p in (0, 1)]
        wmod_s = h2T[:, 0, 0:KD * NM].rearrange("p (k n) -> p k n", k=KD)
        comb = sb("comb", [P, B * NT, EA])
        ident = sb("ident", [P, P])
        ident_bf = sb("ident_bf", [P, P], BF16)
        causal = sb("causal", [P, P], BF16)
        before = sb("before", [P, N_GROUP, N_GROUP])
        wT_s = sb("wT_s", [P, KD, 2 * D])
        gateT_s = sb("gateT_s", [P, KD, E])
        bias_s = sb("bias_s", [P, E])
        cT_s = sb("cT_s", [P, KD, B])
        silu_c = sb("silu_c", [P, KD, B])
        sig_c = sb("sig_c", [P, KD, B])
        mod = sb("mod", [B, NM])
        sign = sb("sign", [B, 2, D])
        modT = sb("modT", [P, 6 * KD, B])
        bc = [sb(f"bc{p}", [P, 6, D]) for p in (0, 1)]
        half = sb("half", [P, NT])
        st = sb("st", [P, NT, 6])
        mv = sb("mv", [P, NT, 2])
        veps = sb("veps", [P, NT])
        rstd = sb("rstd", [P, NT])
        st2 = sb("st2", [P, NT, 6])
        mv2 = sb("mv2", [P, NT, 2])
        veps2 = sb("veps2", [P, NT])
        rstd2 = sb("rstd2", [P, NT])
        xn = sb("xn", [P, NT, D])
        xn2 = sb("xn2", [P, NT, D])
        h = [sb(f"h{p}", [P, NT, D]) for p in (0, 1)]
        hT = [sb(f"hT{p}", [P, KD, S]) for p in (0, 1)]
        KT = [sb(f"KT{p}", [P, KD, S]) for p in (0, 1)]
        V = [sb(f"V{p}", [P, NT, D]) for p in (0, 1)]
        probs = [sb(f"probs{p}", [P, S]) for p in (0, 1)]
        pT_s = [sb(f"pT_s{p}", [P, NT, P]) for p in (0, 1)]
        negmax = sb("negmax", [P, NT])
        rowsum = sb("rowsum", [P, NT])
        rinv = sb("rinv", [P, NT])
        t1 = sb("t1", [P, D])
        t2 = [sb(f"t2{p}", [P, D]) for p in (0, 1)]
        esig = sb("esig", [P, NT, E])
        esig1 = sb("esig1", [P, NT, E])
        scores = sb("scores", [P, NT, E])
        sfc = sb("sfc", [P, NT, E])
        gs = sb("gs", [P, NT, N_GROUP])
        cgt = sb("cgt", [P, NT, N_GROUP, N_GROUP])
        ceq = sb("ceq", [P, NT, N_GROUP, N_GROUP])
        ceq2 = sb("ceq2", [P, NT, N_GROUP, N_GROUP])
        cgt2 = sb("cgt2", [P, NT, N_GROUP, N_GROUP])
        rank = sb("rank", [P, NT, N_GROUP])
        gm = sb("gm", [P, NT, N_GROUP])
        masked = sb("masked", [P, NT, E + 2])
        m8 = sb("m8", [P, NT, 8])
        rl = sb("rl", [P, NT, 8])
        after = sb("after", [P, NT, E + 2])
        sel = sb("sel", [P, NT, E])
        tw = sb("tw", [P, NT, E])
        tsum = sb("tsum", [P, NT])
        tinv = sb("tinv", [P, NT])
        gu_s = [sb(f"gu{p}", [P, KD, 2 * I]) for p in (0, 1)]
        dn_s = [sb(f"dn{p}", [P, D]) for p in (0, 1)]
        sg = [pT_s[p][:].rearrange("p a d -> p (a d)") for p in (0, 1)]
        hm = probs
        mod_dram = nc.dram_tensor("mod_dram", [B, NM], F32)

        bank = [ctx.enter_context(nc.psum_tensor(f"bank{i}", [P, 512], F32)) for i in range(8)]

        x_loaded = [sem("x_loaded0"), sem("x_loaded1")]
        w_loaded = sem("w_loaded")
        mod_stored = sem("mod_stored")
        bc_loaded = [sem("bc_loaded0"), sem("bc_loaded1")]
        gb_loaded = sem("gb_loaded")
        out_stored = sem("out_stored")
        pool_const = sem("pool_const")
        consts_ready = sem("consts_ready")
        exp_c_ready = sem("exp_c_ready")
        silu_c_steps = sem("silu_c_steps")
        mod_mm = sem("mod_mm")
        mod_steps = sem("mod_steps")
        mod_ready = sem("mod_ready")
        modT_ready = sem("modT_ready")
        front_steps = sem("front_steps")
        attend_steps = sem("attend_steps")
        back_steps = sem("back_steps")
        norm2_steps = sem("norm2_steps")
        tinv_ready = sem("tinv_ready")
        moments_ready = sem("moments_ready")
        veps_ready = sem("veps_ready")
        rstd_ready = sem("rstd_ready")
        xn_ready = sem("xn_ready")
        xn_turned = sem("xn_turned")
        hT_ready = sem("hT_ready")
        h_scaled = sem("h_scaled")
        h_ready = sem("h_ready")
        kt_mm = sem("kt_mm")
        KT_ready = sem("KT_ready")
        v_mm = sem("v_mm")
        V_ready = sem("V_ready")
        scored = sem("scored")
        max_ready = sem("max_ready")
        probs_ready = sem("probs_ready")
        probs_turned = sem("probs_turned")
        pT_ready = sem("pT_ready")
        attended = sem("attended")
        o_scaled = sem("o_scaled")
        o_gated = sem("o_gated")
        x2_ready = sem("x2_ready")
        moments2_ready = sem("moments2_ready")
        veps2_ready = sem("veps2_ready")
        rstd2_ready = sem("rstd2_ready")
        xn2_ready = sem("xn2_ready")
        xn2_turned = sem("xn2_turned")
        h2T_ready = sem("h2T_ready")
        logits_mm = sem("logits_mm")
        esig_ready = sem("esig_ready")
        gu_loaded = [sem("gu_loaded0"), sem("gu_loaded1")]
        dn_loaded = [sem("dn_loaded0"), sem("dn_loaded1")]
        expert_done = sem("expert_done")
        gate_mm = sem("gate_mm")
        silu_ready = sem("silu_ready")
        hm_ready = sem("hm_ready")
        down_mm = sem("down_mm")
        summed = sem("summed")
        gated_ready = sem("gated_ready")
        y_ready = sem("y_ready")
        waits_apart = sem("waits_apart")

        def run_batches(eng, front, attention, back):
            front(0, 0, 0)
            with eng.Fori(0, B // 2 - 1) as m:
                attention(2 * m, m, 0)
                front(2 * m + 1, m, 1)
                back(2 * m, m, 0)
                attention(2 * m + 1, m, 1)
                front(2 * m + 2, m + 1, 0)
                back(2 * m + 1, m, 1)
            M = B // 2 - 1
            attention(B - 2, M, 0)
            front(B - 1, M, 1)
            back(B - 2, M, 0)
            attention(B - 1, M, 1)
            back(B - 1, M, 1)

        def chain(eng, steps, base):
            done = [0]

            def link(ins):
                done[0] += 1
                ins.then_inc(steps, 1)
                eng.wait_ge(steps, base + done[0])
            return link

        def tile_of(buf, b, i):
            return buf[:, bass.ds(NT * b + i, 1), :].rearrange("p a d -> p (a d)")

        def apart(eng):
            eng.sem_inc(waits_apart, 1)

        block = ctx.enter_context(nc.Block())

        @block.sync
        def _(sp):
            for dst, src in ((cT_s, cT), (wT_s, wT), (gateT_s, gateT)):
                sp.dma_start(dst[:], src.rearrange("(k p) n -> p k n", p=P)).then_inc(w_loaded, 16)
            sp.dma_start(wmod_s, wmod.rearrange("(k p) n -> p k n", p=P)).then_inc(w_loaded, 16)
            sp.dma_start(bias_s[:], bias.partition_broadcast(P)).then_inc(w_loaded, 16)
            for b in range(B):
                if b >= 2:
                    sp.wait_ge(x_loaded[b % 2], 16 * (b // 2))
                sp.dma_start(xs[:, NT * b:NT * (b + 1), :],
                             x[b].rearrange("(t p) d -> p t d", p=P)).then_inc(x_loaded[b % 2], 16)
            sp.wait_ge(mod_ready, 1)
            sp.dma_start(mod_dram[:, :], mod[:]).then_inc(mod_stored, 16)
            sp.wait_ge(mod_stored, 16)
            for b in range(2):
                sp.dma_start(bc[b][:].rearrange("p a d -> p (a d)"), mod_dram[b].partition_broadcast(P)).then_inc(bc_loaded[b], 16)
            for e in range(2):
                sp.dma_start(gu_s[e][:], guT[e].rearrange("(k p) n -> p k n", p=P)).then_inc(gu_loaded[e], 16)
                sp.dma_start(dn_s[e][:], dnT[e]).then_inc(dn_loaded[e], 16)
            with sp.Fori(1, B // 2) as m:
                for p in (0, 1):
                    sp.wait_ge(o_gated, NT * (2 * m + p - 1))
                    apart(sp)
                    sp.wait_ge(bc_loaded[p], 16 * m)
                    apart(sp)
                    sp.dma_start(bc[p][:].rearrange("p a d -> p (a d)"),
                                 mod_dram[bass.ds(2 * m + p, 1), :].rearrange("a n -> (a n)").partition_broadcast(P)
                                 ).then_inc(bc_loaded[p], 16)
            sp.wait_ge(o_gated, NT * B)
            for p in (0, 1):
                sp.dma_start(h[p][:], mod_dram[p * NT:(p + 1) * NT, GB * D:].partition_broadcast(P)).then_inc(gb_loaded, 16)
            with sp.Fori(1, EA // 2) as m:
                for p in (0, 1):
                    sp.wait_ge(expert_done, 2 * m + p - 1)
                    apart(sp)
                    sp.wait_ge(gu_loaded[p], 16 * m)
                    apart(sp)
                    sp.wait_ge(dn_loaded[p], 16 * m)
                    apart(sp)
                    sp.dma_start(gu_s[p][:], guT[bass.ds(2 * m + p, 1)].rearrange("a (k p) n -> p (a k) n", p=P)
                                 ).then_inc(gu_loaded[p], 16)
                    sp.dma_start(dn_s[p][:], dnT[bass.ds(2 * m + p, 1)].rearrange("a i d -> (a i) d")
                                 ).then_inc(dn_loaded[p], 16)
            for b in range(B):
                sp.wait_ge(y_ready, b + 1)
                sp.dma_start(out[b].rearrange("(t p) d -> p t d", p=P),
                             acc[:, NT * b:NT * (b + 1), :]).then_inc(out_stored, 16)
            sp.wait_ge(out_stored, 16 * B)

        @block.gpsimd
        def _(pool):
            g = nc.gpsimd
            g.memset(ident[:], 0.0).then_inc(pool_const, 1)
            g.memset(causal[:], 0.0).then_inc(pool_const, 1)
            g.memset(before[:], 1.0).then_inc(pool_const, 1)
            g.memset(half[:], -0.5)
            g.memset(masked[:, :, E:E + 2], SENTINEL)
            g.memset(rl[:], SENTINEL)
            pool.wait_ge(pool_const, 3)
            g.affine_select(out=ident[:], in_=ident[:], compare_op=ALU.not_equal, fill=1.0, base=0,
                            pattern=[[-1, P]], channel_multiplier=1).then_inc(pool_const, 1)
            g.affine_select(out=causal[:], in_=causal[:], compare_op=ALU.is_ge, fill=MASKED, base=0,
                            pattern=[[-1, P]], channel_multiplier=1)
            g.affine_select(out=before[:], in_=before[:], compare_op=ALU.is_gt, fill=0.0, base=0,
                            pattern=[[1, N_GROUP], [-1, N_GROUP]], channel_multiplier=0)
            pool.wait_ge(pool_const, 4)
            g.tensor_copy(ident_bf[:], ident[:])
            g.memset(comb[:, :, E:EA], 1.0)
            g.memset(acc[:], 0.0).then_inc(consts_ready, 1)

            def front(b, m, p):
                pool.wait_ge(moments_ready, NT * b + NT)
                apart(pool)
                g.tensor_scalar(veps[:], mv[:, :, 1], LN_EPS, 0.0, ALU.add, ALU.add).then_inc(veps_ready, 1)
                pool.wait_ge(veps_ready, b + 1)
                g.tensor_tensor(rstd[:], veps[:], half[:], ALU.pow).then_inc(rstd_ready, 1)
                pool.wait_ge(xn_ready, b + 1)
                pool.wait_ge(bc_loaded[p], 16 * (m + 1))
                for t in range(NT):
                    last = g.tensor_tensor(h[p][:, t, :], xn[:, t, :], bc[p][:, CA, :], ALU.mult)
                last.then_inc(h_scaled, 1)
                pool.wait_ge(h_scaled, b + 1)
                for t in range(NT):
                    last = g.tensor_tensor(h[p][:, t, :], h[p][:, t, :], bc[p][:, SA, :], ALU.add)
                last.then_inc(h_ready, 1)

            def attention(b, m, p):
                for i in range(NT):
                    pool.wait_ge(o_gated, NT * b + i + 1)
                    g.tensor_tensor(tile_of(xs, b, i), tile_of(xs, b, i), t2[i % 2][:], ALU.add
                                    ).then_inc(x2_ready, 1)

            def back(b, m, p):
                pool.wait_ge(moments2_ready, NT * b + NT)
                apart(pool)
                g.tensor_scalar(veps2[:], mv2[:, :, 1], LN_EPS, 0.0, ALU.add, ALU.add).then_inc(veps2_ready, 1)
                pool.wait_ge(veps2_ready, b + 1)
                g.tensor_tensor(rstd2[:], veps2[:], half[:], ALU.pow).then_inc(rstd2_ready, 1)

            run_batches(pool, front, attention, back)

        @block.tensor
        def _(pe):
            mm = nc.tensor.matmul

            pe.wait_ge(silu_c_steps, 3)
            for c in range(NM // 512):
                for k in range(KD):
                    mm(bank[c][0:B, :], silu_c[:, k, :], wmod_s[:, k, 512 * c:512 * (c + 1)],
                       start=(k == 0), stop=(k == KD - 1))
            for c in range(NM // P):
                for k in range(KD):
                    last = mm(bank[3][:, B * c:B * (c + 1)], wmod_s[:, k, P * c:P * (c + 1)], silu_c[:, k, :],
                              start=(k == 0), stop=(k == KD - 1))
            last.then_inc(mod_mm, 1)

            def front(b, m, p):
                if isinstance(b, int) and b == 0:
                    pe.wait_ge(mod_ready, 1)
                    pe.wait_ge(modT_ready, 1)
                    pe.wait_ge(consts_ready, 1)
                pe.wait_ge(xn_ready, b + 1)
                for k in range(KD):
                    for t in range(NT):
                        last = nc.tensor.transpose(bank[k][:, P * t:P * (t + 1)], xn[:, t, P * k:P * (k + 1)], ident[:])
                    last.then_inc(xn_turned, 1)
                pe.wait_ge(hT_ready, KD * b + KD)
                for c in range(KD):
                    for k in range(KD):
                        last = mm(bank[2 + c][:], wT_s[:, k, P * c:P * (c + 1)], hT[p][:, k, :],
                                  start=(k == 0), stop=(k == KD - 1))
                    last.then_inc(kt_mm, 1)
                for t in range(NT):
                    if t % 2 == 0:
                        pe.wait_ge(KT_ready, KD * b + t // 2 + 1)
                    for k in range(KD):
                        last = mm(bank[2 + t // 2][:, D * (t % 2):D * (t % 2 + 1)], hT[p][:, k, P * t:P * (t + 1)],
                                  wT_s[:, k, D:2 * D], start=(k == 0), stop=(k == KD - 1))
                    if t % 2 == 1:
                        last.then_inc(v_mm, 1)

            def attention(b, m, p):
                def score(i):
                    keys = P * (i + 1)
                    for k in range(KD):
                        mm(bank[4 + i % 2][:, 0:keys], hT[p][:, k, P * i:P * (i + 1)], KT[p][:, k, 0:keys],
                           start=(k == 0), stop=False)
                    mm(bank[4 + i % 2][:, P * i:keys], ident_bf[:], causal[:], start=False, stop=True
                       ).then_inc(scored, 1)

                def turn(i):
                    pe.wait_ge(probs_ready, NT * b + i + 1)
                    for j in range(i + 1):
                        last = nc.tensor.transpose(bank[6][:, P * j:P * (j + 1)], probs[i % 2][:, P * j:P * (j + 1)],
                                                   ident[:])
                    last.then_inc(probs_turned, 1)

                def attend(i):
                    pe.wait_ge(pT_ready, NT * b + i + 1)
                    if i == 0:
                        pe.wait_ge(V_ready, 2 * b + 2)
                    else:
                        pe.wait_ge(o_scaled, NT * b + i)
                    for j in range(i + 1):
                        last = mm(bank[7][:, 0:D], pT_s[i % 2][:, j, :], V[p][:, j, :], start=(j == 0), stop=(j == i))
                    last.then_inc(attended, 1)

                score(0)
                score(1)
                for i in range(NT):
                    turn(i)
                    if i + 2 < NT:
                        score(i + 2)
                    attend(i)

            def back(b, m, p):
                pe.wait_ge(xn2_ready, b + 1)
                for k in range(KD):
                    for t in range(NT):
                        last = nc.tensor.transpose(bank[k][:, P * t:P * (t + 1)], xn2[:, t, P * k:P * (k + 1)], ident[:])
                    last.then_inc(xn2_turned, 1)
                pe.wait_ge(h2T_ready, KD * b + KD)
                for t in range(NT):
                    for k in range(KD):
                        last = mm(bank[7][:, E * t:E * (t + 1)], h2T_s[p][:, k, P * t:P * (t + 1)], gateT_s[:, k, :],
                                  start=(k == 0), stop=(k == KD - 1))
                last.then_inc(logits_mm, 1)

            run_batches(pe, front, attention, back)

            def experts(m, p):
                e8 = B * (2 * m + p)
                pe.wait_ge(gu_loaded[p], 16 * (m + 1))
                pe.wait_ge(dn_loaded[p], 16 * (m + 1))

                def up(s):
                    for c in range(2):
                        for k in range(KD):
                            last = mm(bank[2 * c + s % 2][:], gu_s[p][:, k, I * c:I * (c + 1)],
                                      h2T[:, k, S * s:S * (s + 1)], start=(k == 0), stop=(k == KD - 1))
                    last.then_inc(gate_mm, 1)

                def down(s):
                    pe.wait_ge(hm_ready, e8 + s + 1)
                    if s >= 2:
                        pe.wait_ge(summed, e8 + s - 1)
                    for t in range(NT):
                        last = mm(bank[4 + 2 * (s % 2) + t // 2][:, D * (t % 2):D * (t % 2 + 1)],
                                  hm[s % 2][:, P * t:P * (t + 1)], dn_s[p][:], start=True, stop=True)
                    last.then_inc(down_mm, 1)
                    return last

                up(0)
                for s in range(B):
                    if s + 1 < B:
                        up(s + 1)
                    last = down(s)
                pe.wait_ge(summed, e8 + B)
                pe.sem_inc(expert_done, 1)
            with pe.Fori(0, EA // 2) as m:
                for p in (0, 1):
                    experts(m, p)

        @block.scalar
        def _(act):
            a = nc.scalar.activation
            act.wait_ge(w_loaded, 16 * 5)
            a(sig_c[:], cT_s[:], ACT.Exp, scale=-1.0).then_inc(exp_c_ready, 1)

            def front(b, m, p):
                if isinstance(b, int) and b == 0:
                    act.wait_ge(modT_ready, 1)
                for k in range(KD):
                    act.wait_ge(xn_turned, KD * b + k + 1)
                    a(hT[p][:, k, :], bank[k][:], ACT.Identity, bias=modT[:, SA * KD + k, bass.ds(b, 1)],
                      scale=modT[:, CA * KD + k, bass.ds(b, 1)]).then_inc(hT_ready, 1)
                for c in range(KD):
                    act.wait_ge(kt_mm, KD * b + c + 1)
                    nc.scalar.copy(KT[p][:, c, :], bank[2 + c][:]).then_inc(KT_ready, 1)

            def attention(b, m, p):
                for i in range(NT):
                    keys = P * (i + 1)
                    act.wait_ge(max_ready, NT * b + i + 1)
                    if i >= 2:
                        act.wait_ge(probs_turned, NT * b + i - 1)
                    a(probs[i % 2][:, 0:keys], bank[4 + i % 2][:, 0:keys], ACT.Exp, bias=negmax[:, i:i + 1],
                      accum_out=rowsum[:, i:i + 1]).then_inc(probs_ready, 1)

            def back(b, m, p):
                for k in range(KD):
                    act.wait_ge(xn2_turned, KD * b + k + 1)
                    a(h2T_s[p][:, k, :], bank[k][:], ACT.Identity, bias=modT[:, SB * KD + k, bass.ds(b, 1)],
                      scale=modT[:, CB * KD + k, bass.ds(b, 1)]).then_inc(h2T_ready, 1)
                act.wait_ge(logits_mm, b + 1)
                a(esig[:].rearrange("p t e -> p (t e)"), bank[7][:, 0:NT * E], ACT.Exp, scale=-1.0
                  ).then_inc(esig_ready, 1)

            run_batches(act, front, attention, back)

            with act.Fori(0, EA) as e:
                for s in range(B):
                    act.wait_ge(gate_mm, B * e + s + 1)
                    if s >= 2:
                        act.wait_ge(hm_ready, B * e + s - 1)
                    a(sg[s % 2], bank[s % 2][:], ACT.Silu).then_inc(silu_ready, 1)

        @block.vector
        def _(dve):
            v = nc.vector
            dve.wait_ge(exp_c_ready, 1)
            link = chain(dve, silu_c_steps, 0)
            link(v.tensor_scalar(sig_c[:], sig_c[:], 1.0, None, ALU.add))
            link(v.reciprocal(sig_c[:], sig_c[:]))
            v.tensor_tensor(silu_c[:], sig_c[:], cT_s[:], ALU.mult).then_inc(silu_c_steps, 1)
            dve.wait_ge(mod_mm, 1)
            v.tensor_copy(modT[:].rearrange("p n b -> p (n b)"), bank[3][:, 0:6 * KD * B]).then_inc(mod_steps, 1)
            for c in range(NM // 512):
                last = v.tensor_copy(mod[:, 512 * c:512 * (c + 1)], bank[c][0:B, :])
            last.then_inc(mod_steps, 1)
            dve.wait_ge(mod_steps, 2)
            for n in (CA, CB):
                v.tensor_scalar(mod[:, D * n:D * (n + 1)], mod[:, D * n:D * (n + 1)], 1.0, None, ALU.add)
                last = v.tensor_scalar(modT[:, KD * n:KD * (n + 1), :], modT[:, KD * n:KD * (n + 1), :], 1.0, None, ALU.add)
            last.then_inc(modT_ready, 1)
            gates = [(sign[:, j, :], mod[:, D * n:D * (n + 1)]) for j, n in enumerate((GA, GB))]
            for twice, gate in gates:
                last = v.tensor_scalar(twice, gate, 0.0, 2.0, ALU.is_ge, ALU.mult)
            last.then_inc(mod_steps, 1)
            dve.wait_ge(mod_steps, 3)
            for twice, gate in gates:
                last = v.scalar_tensor_tensor(out=gate, in0=twice, scalar=1.0, in1=gate, op0=ALU.subtract, op1=ALU.mult)
            last.then_inc(mod_steps, 1)
            dve.wait_ge(mod_steps, 4)
            for twice, gate in gates:
                last = v.tensor_scalar(gate, gate, MIN_GATE, None, ALU.max)
            last.then_inc(mod_steps, 1)
            dve.wait_ge(mod_steps, 5)
            for twice, gate in gates:
                last = v.scalar_tensor_tensor(out=gate, in0=twice, scalar=1.0, in1=gate, op0=ALU.subtract, op1=ALU.mult)
            last.then_inc(mod_ready, 1)

            def normalise(b, src, stats, mvs, ready, rstds, rstd_sem, dst, dst_sem, steps):
                link = chain(dve, steps, b)
                apart(dve)
                for t in range(NT):
                    last = v.bn_stats(stats[:, t, :], tile_of(src, b, t))
                link(last)
                apart(dve)
                for t in range(NT):
                    v.bn_aggr(mvs[:, t, :], stats[:, t, :]).then_inc(ready, 1)
                dve.wait_ge(rstd_sem, b + 1)
                for t in range(NT):
                    last = v.tensor_scalar(dst[:, t, :], tile_of(src, b, t), mvs[:, t, 0:1], rstds[:, t:t + 1],
                                           ALU.subtract, ALU.mult)
                last.then_inc(dst_sem, 1)

            def front(b, m, p):
                dve.wait_ge(x_loaded[p], 16 * (m + 1))
                normalise(b, xs, st, mv, moments_ready, rstd, rstd_ready, xn, xn_ready, front_steps)
                for c in range(2):
                    dve.wait_ge(v_mm, 2 * b + c + 1)
                    v.tensor_copy(V[p][:, 2 * c:2 * c + 2, :].rearrange("p a d -> p (a d)"), bank[2 + c][:]
                                  ).then_inc(V_ready, 1)

            def attention(b, m, p):
                def row_max(i):
                    dve.wait_ge(scored, NT * b + i + 1)
                    v.tensor_reduce(negmax[:, i:i + 1], bank[4 + i % 2][:, 0:P * (i + 1)], AX.X, ALU.max, negate=True
                                    ).then_inc(max_ready, 1)

                def copy_turned(i):
                    dve.wait_ge(probs_turned, NT * b + i + 1)
                    v.tensor_copy(pT_s[i % 2][:, 0:i + 1, :].rearrange("p a d -> p (a d)"), bank[6][:, 0:P * (i + 1)]
                                  ).then_inc(pT_ready, 1)

                link = chain(dve, attend_steps, NT * b)

                def output(i):
                    link(v.reciprocal(rinv[:, i:i + 1], rowsum[:, i:i + 1]))
                    if i == 0:
                        dve.wait_ge(h_ready, b + 1)
                    dve.wait_ge(attended, NT * b + i + 1)
                    v.scalar_tensor_tensor(out=t1[:], in0=bank[7][:, 0:D], scalar=rinv[:, i:i + 1], in1=h[p][:, i, :],
                                           op0=ALU.mult, op1=ALU.add).then_inc(o_scaled, 1)
                    dve.wait_ge(o_scaled, NT * b + i + 1)
                    if i >= 2:
                        dve.wait_ge(x2_ready, NT * b + i - 1)
                    v.tensor_tensor(t2[i % 2][:], t1[:], bc[p][:, GA, :], ALU.mult).then_inc(o_gated, 1)

                row_max(0)
                row_max(1)
                for i in range(NT):
                    copy_turned(i)
                    if i + 2 < NT:
                        row_max(i + 2)
                    output(i)

            def back(b, m, p):
                dve.wait_ge(x2_ready, NT * b + NT)
                normalise(b, xs, st2, mv2, moments2_ready, rstd2, rstd2_ready, xn2, xn2_ready, norm2_steps)
                for k in range(KD):
                    dve.wait_ge(h2T_ready, KD * b + k + 1)
                    last = v.tensor_copy(h2T[:, k, bass.ds(b * S, S)], h2T_s[p][:, k, :])
                STEPS = 17
                link = chain(dve, back_steps, STEPS * b)
                dve.wait_ge(esig_ready, b + 1)
                link(v.tensor_scalar(esig1[:], esig[:], 1.0, None, ALU.add))
                link(v.reciprocal(scores[:], esig1[:]))
                link(v.tensor_tensor(sfc[:], scores[:], bias_s[:].rearrange("p (a e) -> p a e", a=1).to_broadcast([P, NT, E]), ALU.add))
                link(v.tensor_reduce(gs[:], sfc[:].rearrange("p t (g e) -> p t g e", e=EG), AX.X, ALU.max))
                for t in range(NT):
                    other = gs[:, t, :].rearrange("p (a g) -> p a g", a=1).to_broadcast([P, N_GROUP, N_GROUP])
                    this = gs[:, t, :].rearrange("p (g a) -> p g a", a=1).to_broadcast([P, N_GROUP, N_GROUP])
                    v.tensor_tensor(cgt[:, t], other, this, ALU.is_gt)
                    last = v.tensor_tensor(ceq[:, t], other, this, ALU.is_equal)
                link(last)
                for t in range(NT):
                    last = v.tensor_tensor(ceq2[:, t], ceq[:, t], before[:], ALU.mult)
                link(last)
                link(v.tensor_tensor(cgt2[:], cgt[:], ceq2[:], ALU.add))
                link(v.tensor_reduce(rank[:], cgt2[:], AX.X, ALU.add))
                link(v.tensor_scalar(gm[:], rank[:], float(TOPK_GROUP), None, ALU.is_lt))
                for t in range(NT):
                    last = v.tensor_tensor(masked[:, t, 0:E].rearrange("p (g e) -> p g e", e=EG),
                                           sfc[:, t, :].rearrange("p (g e) -> p g e", e=EG),
                                           gm[:, t, :].rearrange("p (g a) -> p g a", a=1).to_broadcast([P, N_GROUP, EG]),
                                           ALU.mult)
                link(last)
                apart(dve)
                for t in range(NT):
                    last = v.max(m8[:, t, :], masked[:, t, 0:E])
                link(last)
                link(v.tensor_copy(rl[:, :, 0:TOP_K], m8[:, :, 0:TOP_K]))
                apart(dve)
                for t in range(NT):
                    last = v.match_replace(after[:, t, :], rl[:, t, :], masked[:, t, :], TAKEN)
                link(last)
                link(v.tensor_tensor(sel[:], after[:, :, 0:E], masked[:, :, 0:E], ALU.not_equal))
                link(v.tensor_tensor(tw[:], sel[:], scores[:], ALU.mult))
                link(v.tensor_reduce(tsum[:], tw[:], AX.X, ALU.add))
                link(v.tensor_scalar(tsum[:], tsum[:], 1e-20, None, ALU.add))
                v.reciprocal(tinv[:], tsum[:]).then_inc(tinv_ready, 1)
                dve.wait_ge(tinv_ready, b + 1)
                for t in range(NT):
                    v.tensor_scalar(comb[:, bass.ds(NT * b + t, 1), 0:E].rearrange("p a e -> p (a e)"), tw[:, t, :],
                                    tinv[:, t:t + 1], ROUTE_SCALE, ALU.mult, ALU.mult)
            run_batches(dve, front, attention, back)

            with dve.Fori(0, EA) as e:
                def gated(s):
                    dve.wait_ge(silu_ready, B * e + s + 1)
                    v.tensor_tensor(hm[s % 2][:], sg[s % 2], bank[2 + s % 2][:], ALU.mult).then_inc(hm_ready, 1)

                def add_up(s):
                    dve.wait_ge(down_mm, B * e + s + 1)
                    for t in range(NT):
                        n = NT * s + t
                        last = v.scalar_tensor_tensor(
                            out=acc[:, n, :], in0=bank[4 + 2 * (s % 2) + t // 2][:, D * (t % 2):D * (t % 2 + 1)],
                            scalar=comb[:, n, bass.ds(e, 1)], in1=acc[:, n, :], op0=ALU.mult, op1=ALU.add)
                    last.then_inc(summed, 1)

                for s in range(B):
                    gated(s)
                    if s:
                        add_up(s - 1)
                add_up(B - 1)
            dve.wait_ge(gb_loaded, 32)
            for b in range(B):
                for t in range(NT):
                    last = v.tensor_tensor(acc[:, NT * b + t, :], acc[:, NT * b + t, :], h[b // NT][:, b % NT, :], ALU.mult)
                last.then_inc(gated_ready, 1)
                dve.wait_ge(gated_ready, b + 1)
                v.tensor_tensor(acc[:, NT * b:NT * (b + 1), :], acc[:, NT * b:NT * (b + 1), :],
                                xs[:, NT * b:NT * (b + 1), :], ALU.add).then_inc(y_ready, 1)


def kernel(**inputs):
    import numpy as np
    import concourse.bacc as bacc
    from concourse import mybir as mb
    from concourse.bass_utils import run_bass_kernel_spmd as run

    f = {k: np.asarray(a) for k, a in inputs.items()}
    I = f["L0_ffn_experts_down"].shape[2]
    D = f["L0_ffn_experts_down"].shape[1]
    gate, up, down = (f[f"L0_ffn_shared_{n}_w"] for n in ("gate", "up", "down"))
    shared_gu = np.concatenate([gate.reshape(-1, I, D), up.reshape(-1, I, D)], axis=1)
    gu = np.concatenate([f["L0_ffn_experts_gate_up"], shared_gu], axis=0)
    dn = np.concatenate([f["L0_ffn_experts_down"].transpose(0, 2, 1), down.T.reshape(-1, I, D)], axis=0)
    arrays = {
        "x": f["L0_attn_x"], "wT": f["L0_attn_W"].T, "gateT": f["L0_ffn_gate_weight"].T,
        "bias": f["L0_ffn_e_score_correction_bias"], "guT": gu.transpose(0, 2, 1), "dnT": dn,
        "cT": f["L0_c"].T, "wmod": f["L0_wmod"],
    }
    arrays = {k: np.ascontiguousarray(a) for k, a in arrays.items()}
    nc = bacc.Bacc("TRN2", target_bir_lowering=False, num_devices=1)
    args = [nc.dram_tensor(k, a.shape, mb.dt.from_np(a.dtype), kind="ExternalInput").ap() for k, a in arrays.items()]
    out = nc.dram_tensor("out", f["L0_attn_x"].shape, mb.dt.float32, kind="ExternalOutput").ap()
    build_adaln_block(nc, *args, out)
    r = run(nc, [arrays], core_ids=[0])
    return r.results[0]["out"]
```

```python
from contextlib import ExitStack

import concourse.bass as bass
from concourse import mybir

P = 128
ALU = mybir.AluOpType
ACT = mybir.ActivationFunctionType
AX = mybir.AxisListType
F32 = mybir.dt.float32
BF16 = mybir.dt.bfloat16
I32 = mybir.dt.int32
U32 = mybir.dt.uint32

LN_EPS = 1e-5
MIN_GATE = 0.25
MASKED = -1e30
N_GROUP, TOPK_GROUP, TOP_K, ROUTE_SCALE = 8, 4, 6, 2.5
SA, CA, GA, SB, CB, GB = range(6)
RSQRT_SEED = 0x5F3759DF
NEWTON = 3
XG = 8
YT = 8


def build_adaln_block(nc, x, wT, gateT, bias, guT, dnT, sguT, sdnT, cT, wmod, out):
    B, S, D = x.shape
    E = gateT.shape[1]
    I = dnT.shape[1]
    SI = sdnT.shape[0]
    KD = D // P
    KI = SI // P
    NT = S // P
    T = B * S
    NM = 6 * D
    EG = E // N_GROUP
    CAP = T + P
    ROWS = E * CAP + P
    ROW = D + 3 * TOP_K
    BLOCKS = T * TOP_K // P + E
    NH = -(-BLOCKS // P)

    with ExitStack() as ctx:
        def sb(name, shape, dt=F32):
            return ctx.enter_context(nc.sbuf_tensor(name, shape, dt))

        def sem(name):
            return ctx.enter_context(nc.semaphore(name))

        xs = sb("xs", [P, B * NT, D])
        gu_s = sb("gu_s", [P, KD, E, 2 * I])
        dn_s = sb("dn_s", [P, E, D])
        sgu_s = sb("sgu_s", [P, KD, 2 * SI])
        sdn_s = sb("sdn_s", [P, KI, D])
        gb_all = sb("gb_all", [P, B, D])
        ident = sb("ident", [P, P])
        ident_bf = sb("ident_bf", [P, P], BF16)
        causal = sb("causal", [P, P], BF16)
        earlier = sb("earlier", [P, P], BF16)
        ones_bf = sb("ones_bf", [P, P], BF16)
        upto = sb("upto", [E, E])
        before = sb("before", [P, N_GROUP, N_GROUP])
        experts_iota = sb("experts_iota", [P, E])
        area = sb("area", [P, E])
        block_no = sb("block_no", [P, NH])
        lane = sb("lane", [P, 1])
        base = sb("base", [P, E])
        dest0 = sb("dest_of_token", [P, NT, TOP_K])
        taken = [0]

        def early(free, parts=P):
            view = dn_s[:].rearrange("p e d -> p (e d)")[0:parts, taken[0]:taken[0] + free]
            taken[0] += free
            return view

        wT_s = early(KD * 2 * D).rearrange("p (k n) -> p k n", k=KD)
        mod = early(NM, B)
        sign = early(2 * D, B).rearrange("p (j d) -> p j d", j=2)
        u = [early(D) for n in (0, 1)]
        t1 = early(D)
        t2 = [early(D) for n in (0, 1)]
        probs = [early(S) for p in (0, 1)]
        pT_s = [early(NT * P) for p in (0, 1)]
        gateT_s = sb("gateT_s", [P, KD, E])
        bias_s = sb("bias_s", [P, 1, E])
        cT_s = sb("cT_s", [P, KD, B])
        silu_c = sb("silu_c", [P, KD, B])
        sig_c = sb("sig_c", [P, KD, B])
        bc = [sb(f"bc{p}", [P, 5, D]) for p in (0, 1)]
        pad = sb("pad", [P, ROW])

        st = sb("st", [P, NT, 6])
        mv = sb("mv", [P, NT, 2])
        rs_v, rs_y, rs_a, rs_b, rs_c = (sb(f"rs_{n}", [P, NT]) for n in "vyabc")
        rs_i = sb("rs_i", [P, NT], I32)
        h = [sb(f"h{p}", [P, NT, D]) for p in (0, 1)]
        rows = [sb(f"rows{p}", [P, NT, ROW]) for p in (0, 1)]
        hT = sb("hT", [P, KD, S])
        KT = sb("KT", [P, KD, S])
        V = sb("V", [P, NT, D])
        h2T = sb("h2T", [P, KD, S])
        negmax = sb("negmax", [P, NT])
        rowsum = sb("rowsum", [P, NT])
        rinv = sb("rinv", [P, NT])
        th = sb("th", [P, S])
        sh = sb("sh", [P, KI, S])
        esig = sb("esig", [P, NT, E])
        scores = sb("scores", [P, NT, E])
        sfc = sb("sfc", [P, NT, E])
        gs = sb("gs", [P, NT, N_GROUP])
        eq = sb("eq", [P, NT, TOP_K, E])
        pr = sb("pr", [P, NT, TOP_K, E])
        cgt = eq[:].rearrange("p t j e -> p (t j e)")[:, 0:NT * N_GROUP ** 2].rearrange(
            "p (t g o) -> p t g o", t=NT, g=N_GROUP)
        ceq = pr[:].rearrange("p t j e -> p (t j e)")[:, 0:NT * N_GROUP ** 2].rearrange(
            "p (t g o) -> p t g o", t=NT, g=N_GROUP)
        rank = sb("rank", [P, NT, N_GROUP])
        masked = sb("masked", [P, NT, E])
        m8 = sb("m8", [P, NT, 8])
        i8 = sb("i8", [P, NT, 8], U32)
        idx = sb("idx", [P, NT, TOP_K])
        sel = sb("sel", [P, NT, E], BF16)
        pos = [sb(f"pos{p}", [P, NT, TOP_K], I32) for p in (0, 1)]
        raw = sb("raw", [P, NT, TOP_K])
        tsum = sb("tsum", [P, NT])

        blocks_i = sb("blocks_i", [P, E], I32)
        blocks_f = sb("blocks_f", [P, E])
        blocksT = sb("blocksT", [E, P])
        cum = sb("cum", [P, E])
        cum_ex = sb("cum_ex", [P, E])
        hit = sb("hit", [P, E])
        e_f = sb("e_f", [P, NH])
        skipped = sb("skipped", [P, NH])
        valid = sb("valid", [P, NH])
        r1 = sb("r1", [P, NH])
        r2 = sb("r2", [P, NH])
        table_f = sb("table_f", [P, NH])
        table_e = sb("table_e", [P, NH], I32)
        table_r = sb("table_r", [P, NH], I32)
        base_i = sb("base_i", [P, E], I32)

        expert_row = bc[0][0:1, 0, 0:NH * P].bitcast(I32)
        start_row = bc[0][0:1, 1, 0:NH * P].bitcast(I32)
        expert_bc = bc[0][:, 2, 0:NH * P]

        xg = [rows[n // NT][:, n % NT, :] for n in range(XG)]
        yb = [h[n // NT][:, n % NT, :] for n in range(XG)]
        xgT = [V[:, n, :] for n in (0, 1)]
        sg = [h2T[:, 0, P * n:P * (n + 1)] for n in (0, 1)]
        hs = [h2T[:, 0, P * (n + 2):P * (n + 3)] for n in (0, 1)]
        hsT = [h2T[:, 1, P * n:P * (n + 1)] for n in (0, 1)]
        found = sb("found", [P, XG, 2])
        match = sb("match", [P, 2, 2, TOP_K])
        dest = [sb(f"place{n}", [P, 1], I32) for n in range(XG)]

        wmod_s = gu_s[:, 0, 0:KD * NM // (2 * I), :].rearrange("p a n -> p (a n)").rearrange(
            "p (k n) -> p k n", k=KD)

        mod_dram = nc.dram_tensor("mod_dram", [B, NM], F32)
        sorted_dram = nc.dram_tensor("sorted_dram", [ROWS, ROW], F32)
        y_dram = nc.dram_tensor("y_dram", [T * TOP_K, D], F32)
        expert_dram = nc.dram_tensor("expert_dram", [NH * P], I32)
        start_dram = nc.dram_tensor("start_dram", [NH * P], I32)
        expert_f_dram = nc.dram_tensor("expert_f_dram", [NH * P], F32)

        bank = [ctx.enter_context(nc.psum_tensor(f"bank{i}", [P, 512], F32)) for i in range(8)]

        w_loaded = sem("w_loaded")
        experts_loaded = sem("experts_loaded")
        down_loaded = sem("down_loaded")
        x_loaded = [sem("x_loaded0"), sem("x_loaded1")]
        mod_stored = sem("mod_stored")
        bc_loaded = [sem("bc_loaded0"), sem("bc_loaded1")]
        gb_loaded = sem("gb_loaded")
        pool_const = sem("pool_const")
        consts_ready = sem("consts_ready")
        exp_c_ready = sem("exp_c_ready")
        silu_c_steps = sem("silu_c_steps")
        mod_mm = sem("mod_mm")
        mod_steps = sem("mod_steps")
        mod_ready = sem("mod_ready")
        front_steps = sem("front_steps")
        norm2_steps = sem("norm2_steps")
        attend_steps = sem("attend_steps")
        choose_steps = sem("choose_steps")
        place_steps = sem("place_steps")
        share_steps = sem("share_steps")
        h_ready = sem("h_ready")
        h_turned = sem("h_turned")
        hT_ready = sem("hT_ready")
        kt_mm = sem("kt_mm")
        KT_ready = sem("KT_ready")
        v_mm = sem("v_mm")
        V_ready = sem("V_ready")
        scored = sem("scored")
        max_ready = sem("max_ready")
        probs_ready = sem("probs_ready")
        probs_turned = sem("probs_turned")
        pT_ready = sem("pT_ready")
        attended = sem("attended")
        o_scaled = sem("o_scaled")
        x2_ready = sem("x2_ready")
        h2_ready = sem("h2_ready")
        h2_turned = sem("h2_turned")
        h2T_ready = sem("h2T_ready")
        logits_mm = sem("logits_mm")
        esig_ready = sem("esig_ready")
        eq_ready = sem("eq_ready")
        sel_ready = sem("sel_ready")
        rank_mm = sem("rank_mm")
        rank_read = sem("rank_read")
        pos_ready = sem("pos_ready")
        rows_free = sem("rows_free")
        scattered = [sem("scattered0"), sem("scattered1")]
        share_mm = sem("share_mm")
        tanh_ready = sem("tanh_ready")
        share_hidden = sem("share_hidden")
        share_down = sem("share_down")
        share_added = sem("share_added")
        table_steps = sem("table_steps")
        blocks_ready = sem("blocks_ready")
        blocks_turned = sem("blocks_turned")
        blocksT_ready = sem("blocksT_ready")
        cum_mm = sem("cum_mm")
        table_ready = sem("table_ready")
        table_stored = sem("table_stored")
        table_loaded = sem("table_loaded")
        padded = sem("padded")
        xg_loaded = [sem(f"xg_loaded{n}") for n in range(XG)]
        xg_turned = sem("xg_turned")
        xgT_ready = sem("xgT_ready")
        gu_mm = sem("gu_mm")
        silu_ready = sem("silu_ready")
        hs_ready = sem("hs_ready")
        hs_turned = sem("hs_turned")
        hsT_ready = sem("hsT_ready")
        y_mm = sem("y_mm")
        dest_steps = sem("dest_steps")
        dest_ready = sem("dest_ready")
        y_ready = sem("y_ready")
        y_scattered = [sem(f"y_scattered{n}") for n in range(XG)]
        y_loaded = [sem(f"y_loaded{k}") for k in range(YT)]
        halved = sem("halved")
        added = sem("added")
        summed = sem("summed")
        gated = sem("gated")
        out_ready = sem("out_ready")
        out_stored = sem("out_stored")
        waits_apart = sem("waits_apart")

        def apart(eng):
            eng.sem_inc(waits_apart, 1)

        def run_batches(eng, front, attention):
            front(0, 0, 0)
            attention(0, 0, 0, False, True)
            with eng.Fori(0, B // 2 - 1) as m:
                attention(2 * m + 1, m, 1, True, True)
                attention(2 * m + 2, m + 1, 0, True, True)
            attention(B - 1, B // 2 - 1, 1, True, False)

        def chain(eng, steps, base):
            done = [0]

            def link(ins):
                done[0] += 1
                ins.then_inc(steps, 1)
                eng.wait_ge(steps, base + done[0])
            link.done = done
            return link

        def run_blocks(eng, stages, skew, begin_turn=None):
            deep = max(skew)

            def one(r, q, k):
                for stage, s in zip(stages, skew):
                    if isinstance(r, int) and not 0 <= r - s < BLOCKS:
                        continue
                    stage(r - s, q + (k - s) // XG, (k - s) % XG, k - s)
            begin_turn = begin_turn or (lambda q: None)
            begin_turn(0)
            for r in range(XG):
                one(r, 0, r)
            with eng.Fori(1, BLOCKS // XG) as q:
                begin_turn(q)
                for k in range(XG):
                    one(XG * q + k, q, k)
            if deep:
                begin_turn(BLOCKS // XG)
            for r in range(BLOCKS, BLOCKS + deep):
                one(r, BLOCKS // XG, r - BLOCKS)

        def tile_of(buf, b, i):
            return buf[:, bass.ds(NT * b + i, 1), :].rearrange("p a d -> p (a d)")

        yt_place = gu_s[:].rearrange("p k e n -> p (k e n)")
        yt = [yt_place[:, TOP_K * D * k:TOP_K * D * (k + 1)] for k in range(YT)]
        y3 = [t[:, 0:3 * D] for t in yt]
        y1 = [t[:, 3 * D:4 * D] for t in yt]
        yg = [t[:, 4 * D:5 * D] for t in yt]

        def run_tiles(eng, stages):
            with eng.Fori(0, B * NT // YT) as m:
                for k in range(YT + len(stages) - 1):
                    for s, stage in enumerate(stages):
                        if 0 <= k - s < YT:
                            stage(YT * m + k - s, m, k - s)

        def load_outputs(eng, n, k):
            src = y_dram[bass.ds(n * (P * TOP_K), P * TOP_K), :].rearrange("(p j) d -> p (j d)", j=TOP_K)
            eng.dma_start(yt[k], src).then_inc(y_loaded[k], 16)

        def store_tile(eng, n):
            eng.dma_start(out.rearrange("b s d -> (b s) d")[bass.ds(n * P, P), :], tile_of(xs, 0, n)
                          ).then_inc(out_stored, 16)

        block = ctx.enter_context(nc.Block())

        @block.sync
        def _(sp):
            for dst, src in ((cT_s[:], cT), (wmod_s, wmod), (wT_s, wT), (gateT_s[:], gateT)):
                sp.dma_start(dst, src.rearrange("(k p) n -> p k n", p=P)).then_inc(w_loaded, 16)
            sp.dma_start(bias_s[:, 0, :], bias.partition_broadcast(P)).then_inc(w_loaded, 16)
            for b in range(2):
                sp.dma_start(xs[:, NT * b:NT * (b + 1), :],
                             x[b].rearrange("(t p) d -> p t d", p=P)).then_inc(x_loaded[b % 2], 16)
            sp.wait_ge(mod_ready, 1)
            sp.dma_start(mod_dram[:, :], mod).then_inc(mod_stored, 16)
            sp.wait_ge(mod_stored, 16)
            for b in range(2):
                sp.dma_start(bc[b][:].rearrange("p a d -> p (a d)"), mod_dram[b, 0:GB * D].partition_broadcast(P)
                             ).then_inc(bc_loaded[b], 16)
            sp.dma_start(gb_all[:], mod_dram[:, GB * D:].partition_broadcast(P)).then_inc(gb_loaded, 16)
            for b in range(2, B):
                sp.wait_ge(x_loaded[b % 2], 16 * (b // 2))
                sp.dma_start(xs[:, NT * b:NT * (b + 1), :],
                             x[b].rearrange("(t p) d -> p t d", p=P)).then_inc(x_loaded[b % 2], 16)
            sp.dma_start(sgu_s[:], sguT.rearrange("(k p) n -> p k n", p=P)).then_inc(experts_loaded, 16)
            sp.dma_start(sdn_s[:], sdnT.rearrange("(k p) n -> p k n", p=P)).then_inc(experts_loaded, 16)
            for k in range(KD):
                sp.dma_start(gu_s[:, k], guT[:, P * k:P * (k + 1), :].rearrange("e p n -> p e n")
                             ).then_inc(experts_loaded, 16)
            with sp.Fori(1, B // 2) as m:
                for p in (0, 1):
                    sp.wait_ge(h2_ready, NT * (2 * m + p - 1))
                    apart(sp)
                    sp.wait_ge(bc_loaded[p], 16 * m)
                    apart(sp)
                    sp.dma_start(bc[p][:].rearrange("p a d -> p (a d)"),
                                 mod_dram[bass.ds(2 * m + p, 1), 0:GB * D].rearrange("a n -> (a n)")
                                 .partition_broadcast(P)).then_inc(bc_loaded[p], 16)
            sp.wait_ge(h2_ready, NT * B)
            sp.dma_start(dn_s[:], dnT.rearrange("e p n -> p e n")).then_inc(down_loaded, 16)
            sp.wait_ge(table_ready, 1)
            for dst, src in ((expert_dram, table_e), (start_dram, table_r), (expert_f_dram, table_f)):
                for n in range(NH):
                    sp.dma_start(dst[P * n:P * (n + 1)].rearrange("(p a) -> p a", a=1), src[:, n:n + 1]
                                 ).then_inc(table_stored, 16)
            sp.wait_ge(table_stored, 16 * 3 * NH)
            sp.dma_start(expert_row, expert_dram[:].rearrange("(a n) -> a n", a=1)).then_inc(table_loaded, 16)
            sp.dma_start(start_row, start_dram[:].rearrange("(a n) -> a n", a=1)).then_inc(table_loaded, 16)
            sp.dma_start(expert_bc, expert_f_dram[:].partition_broadcast(P)).then_inc(table_loaded, 16)
            with sp.Fori(0, E) as e:
                first = sp.value_load(base_i[0:1, bass.ds(e, 1)], min_val=0, max_val=ROWS - P)
                sp.dma_start(sorted_dram[bass.ds(first, P), :], pad[:]).then_inc(padded, 16)
            sp.dma_start(sorted_dram[E * CAP:E * CAP + P, :], pad[:]).then_inc(padded, 16)
            sp.wait_ge(padded, 16 * (E + 1))
            for p in (0, 1):
                sp.wait_ge(scattered[p], 16 * NT * TOP_K * (B // 2))
            sp.wait_ge(table_loaded, 16 * 3)

            first_row = {}

            def first_rows_of_turn(q):
                _, regs = nc.values_load_multi_w_load_instructions(
                    start_row[0:1, bass.ds(q * XG, XG)], (mybir.EngineType.SP,), min_val=0, max_val=ROWS - P)
                first_row.update(enumerate(regs))

            def load_rows(i, q, n, at):
                if not (isinstance(i, int) and i < XG):
                    sp.wait_ge(xg_turned, i - XG + 1)
                    apart(sp)
                    sp.wait_ge(dest_ready, i - XG + 1)
                    apart(sp)
                sp.dma_start(xg[n], sorted_dram[bass.ds(first_row[at], P), :]).then_inc(xg_loaded[n], 16)
            run_blocks(sp, [load_rows], [0], first_rows_of_turn)

            for n in range(XG):
                sp.wait_ge(y_scattered[n], 16 * (BLOCKS // XG))
            for k in range(YT):
                load_outputs(sp, k, k)
            with sp.Fori(1, B * NT // YT) as m:
                for k in range(YT):
                    sp.wait_ge(out_ready, YT * (m - 1) + k + 1)
                    apart(sp)
                    load_outputs(sp, YT * m + k, k)
            sp.wait_ge(out_stored, 16 * B * NT)

        @block.gpsimd
        def _(pool):
            g = nc.gpsimd
            iota = dict(allow_small_or_imprecise_dtypes=True)
            g.memset(ident[:], 0.0)
            g.memset(causal[:], 0.0)
            g.memset(before[:], 1.0)
            g.memset(earlier[:], 1.0)
            g.memset(ones_bf[:], 1.0)
            g.memset(upto[:], 1.0).then_inc(pool_const, 1)
            g.iota(experts_iota[:], [[1, E]], base=0, channel_multiplier=0, **iota)
            g.iota(area[:], [[0, 1], [CAP, E]], base=0, channel_multiplier=0, **iota)
            g.iota(block_no[:], [[P, NH]], base=0, channel_multiplier=1, **iota)
            g.iota(dest0[:], [[P * TOP_K, NT], [1, TOP_K]], base=1, channel_multiplier=TOP_K, **iota)
            g.memset(pad[:], 0.0)
            pool.wait_ge(pool_const, 1)
            g.affine_select(out=ident[:], in_=ident[:], compare_op=ALU.not_equal, fill=1.0, base=0,
                            pattern=[[-1, P]], channel_multiplier=1)
            g.affine_select(out=causal[:], in_=causal[:], compare_op=ALU.is_ge, fill=MASKED, base=0,
                            pattern=[[-1, P]], channel_multiplier=1)
            g.affine_select(out=before[:], in_=before[:], compare_op=ALU.is_gt, fill=0.0, base=0,
                            pattern=[[1, N_GROUP], [-1, N_GROUP]], channel_multiplier=0)
            g.affine_select(out=earlier[:], in_=earlier[:], compare_op=ALU.is_gt, fill=0.0, base=0,
                            pattern=[[1, P]], channel_multiplier=-1)
            g.affine_select(out=upto[:], in_=upto[:], compare_op=ALU.is_ge, fill=0.0, base=0,
                            pattern=[[1, E]], channel_multiplier=-1).then_inc(pool_const, 1)
            pool.wait_ge(pool_const, 2)
            g.tensor_copy(base[:], area[:])
            g.tensor_copy(ident_bf[:], ident[:]).then_inc(consts_ready, 1)

            def scatter(b, m, p):
                pool.wait_ge(pos_ready, b + 1)
                apart(pool)
                if not (isinstance(b, int) and b == 0):
                    pool.wait_ge(scattered[1 - p], 16 * NT * TOP_K * (m + p))
                pool.sem_inc(rows_free, 1)
                for t in range(NT):
                    for j in range(TOP_K):
                        g.indirect_dma_start(
                            out=sorted_dram[:, :], out_offset=bass.IndirectOffsetOnAxis(
                                ap=pos[p][:, t, j:j + 1].bitcast(U32), axis=0),
                            in_=rows[p][:, t, :], in_offset=None).then_inc(scattered[p], 16)

            for b in range(2):
                scatter(b, 0, b)
            with pool.Fori(1, B // 2) as m:
                for p in (0, 1):
                    scatter(2 * m + p, m, p)

            def scatter_outputs(i, q, n, at):
                pool.wait_ge(dest_ready, i + 1)
                apart(pool)
                pool.wait_ge(y_ready, i + 1)
                apart(pool)
                g.indirect_dma_start(
                    out=y_dram[:, :], out_offset=bass.IndirectOffsetOnAxis(ap=dest[n][:, 0:1].bitcast(U32), axis=0),
                    in_=yb[n], in_offset=None, bounds_check=T * TOP_K - 1, oob_is_err=False
                    ).then_inc(y_scattered[n], 16)
            run_blocks(pool, [scatter_outputs], [0])

            def third(n, m, k):
                pool.wait_ge(added, n + 1)
                apart(pool)
                g.tensor_tensor(y1[k], y1[k], y3[k][:, 2 * D:3 * D], ALU.add).then_inc(summed, 1)

            def gate(n, m, k):
                pool.wait_ge(summed, n + 1)
                apart(pool)
                g.tensor_tensor(yg[k], y1[k], tile_of(gb_all, 0, YT // NT * m + k // NT), ALU.mult
                                ).then_inc(gated, 1)

            def add_x(n, m, k):
                pool.wait_ge(gated, n + 1)
                apart(pool)
                g.tensor_tensor(tile_of(xs, 0, n), tile_of(xs, 0, n), yg[k], ALU.add).then_inc(out_ready, 1)

            run_tiles(pool, [third, gate, add_x])

        @block.tensor
        def _(pe):
            mm = nc.tensor.matmul

            pe.wait_ge(silu_c_steps, 3)
            for c in range(NM // 512):
                for k in range(KD):
                    last = mm(bank[c][0:B, :], silu_c[:, k, :], wmod_s[:, k, 512 * c:512 * (c + 1)],
                              start=(k == 0), stop=(k == KD - 1))
            last.then_inc(mod_mm, 1)
            pe.wait_ge(consts_ready, 1)

            def front(b, m, p):
                pe.wait_ge(h_ready, NT * b + NT)
                if not (isinstance(b, int) and b < 2):
                    pe.wait_ge(share_added, b - 1)
                for k in range(KD):
                    for t in range(NT):
                        last = nc.tensor.transpose(bank[k][:, P * t:P * (t + 1)], h[p][:, t, P * k:P * (k + 1)],
                                                   ident[:])
                    last.then_inc(h_turned, 1)
                pe.wait_ge(hT_ready, KD * b + KD)
                if not (isinstance(b, int) and b < 2):
                    pe.wait_ge(rank_read, b - 1)
                for c in range(KD):
                    for k in range(KD):
                        last = mm(bank[2 + c][:], wT_s[:, k, P * c:P * (c + 1)], hT[:, k, :],
                                  start=(k == 0), stop=(k == KD - 1))
                    last.then_inc(kt_mm, 1)
                for t in range(NT):
                    if t % 2 == 0:
                        pe.wait_ge(KT_ready, KD * b + t // 2 + 1)
                    for k in range(KD):
                        last = mm(bank[2 + t // 2][:, D * (t % 2):D * (t % 2 + 1)], hT[:, k, P * t:P * (t + 1)],
                                  wT_s[:, k, D:2 * D], start=(k == 0), stop=(k == KD - 1))
                    if t % 2 == 1:
                        last.then_inc(v_mm, 1)

            def share(b, c):
                if c == 0:
                    pe.wait_ge(V_ready, 2 * (b + 1) + 2 if not (isinstance(b, int) and b == B - 1) else 2 * B)
                else:
                    pe.wait_ge(share_hidden, KI * b + c)
                for n in range(2):
                    for k in range(KD):
                        last = mm(bank[2 + n][:], sgu_s[:, k, SI * n + P * c:SI * n + P * (c + 1)], h2T[:, k, :],
                                  start=(k == 0), stop=(k == KD - 1))
                last.then_inc(share_mm, 1)

            def share_out(b):
                pe.wait_ge(share_hidden, KI * b + KI)
                for t in range(NT):
                    for c in range(KI):
                        last = mm(bank[t // 2][:, D * (t % 2):D * (t % 2 + 1)], sh[:, c, P * t:P * (t + 1)],
                                  sdn_s[:, c, :], start=(c == 0), stop=(c == KI - 1))
                last.then_inc(share_down, 1)

            def rank_of(b):
                pe.wait_ge(sel_ready, b + 1)
                flat = sel[:].rearrange("p t e -> p (t e)")
                mm(bank[2][:, 0:NT * E], earlier[:], flat, start=True, stop=False, skip_group_check=True)
                for t in range(1, NT):
                    mm(bank[2][:, E * t:E * NT], ones_bf[:], flat[:, 0:E * (NT - t)], start=False, stop=(t == NT - 1),
                       skip_group_check=True)
                for t in range(NT):
                    last = mm(bank[3][:, 0:E], ones_bf[:], sel[:, t, :], start=(t == 0), stop=(t == NT - 1))
                last.then_inc(rank_mm, 1)

            def attention(b, m, p, late, more):
                def score(i):
                    keys = P * (i + 1)
                    for k in range(KD):
                        mm(bank[4 + i % 2][:, 0:keys], hT[:, k, P * i:P * (i + 1)], KT[:, k, 0:keys],
                           start=(k == 0), stop=False)
                    mm(bank[4 + i % 2][:, P * i:keys], ident_bf[:], causal[:], start=False, stop=True
                       ).then_inc(scored, 1)

                def turn(i):
                    pe.wait_ge(probs_ready, NT * b + i + 1)
                    for j in range(i + 1):
                        last = nc.tensor.transpose(bank[6][:, P * j:P * (j + 1)], probs[i % 2][:, P * j:P * (j + 1)],
                                                   ident[:])
                    last.then_inc(probs_turned, 1)

                def attend(i):
                    pe.wait_ge(pT_ready, NT * b + i + 1)
                    if i == 0:
                        pe.wait_ge(V_ready, 2 * b + 2)
                    else:
                        pe.wait_ge(o_scaled, NT * b + i)
                    for j in range(i + 1):
                        last = mm(bank[7][:, 0:D], pT_s[i % 2][:, P * j:P * (j + 1)], V[:, j, :], start=(j == 0),
                                  stop=(j == i))
                    last.then_inc(attended, 1)

                score(0)
                score(1)
                if late:
                    if isinstance(b, int) and b == 1 or not isinstance(b, int) or b:
                        pe.wait_ge(experts_loaded, 16 * (2 + KD))
                    share(b - 1, 0)
                turn(0)
                score(2)
                attend(0)
                if late:
                    share(b - 1, 1)
                turn(1)
                score(3)
                attend(1)
                if late:
                    share_out(b - 1)
                turn(2)
                attend(2)
                if late:
                    rank_of(b - 1)
                turn(3)
                attend(3)
                if more:
                    front(b + 1, None, 1 - p)
                pe.wait_ge(h2_ready, NT * b + NT)
                if late and not more:
                    pe.wait_ge(share_added, b)
                for k in range(KD):
                    for t in range(NT):
                        last = nc.tensor.transpose(bank[k][:, P * t:P * (t + 1)], rows[p][:, t, P * k:P * (k + 1)],
                                                   ident[:])
                    last.then_inc(h2_turned, 1)
                pe.wait_ge(h2T_ready, KD * b + KD)
                for t in range(NT):
                    for k in range(KD):
                        last = mm(bank[7][:, E * t:E * (t + 1)], h2T[:, k, P * t:P * (t + 1)], gateT_s[:, k, :],
                                  start=(k == 0), stop=(k == KD - 1))
                last.then_inc(logits_mm, 1)

            run_batches(pe, front, attention)
            pe.wait_ge(rank_read, B - 1)
            share(B - 1, 0)
            share(B - 1, 1)
            share_out(B - 1)
            rank_of(B - 1)
            pe.wait_ge(blocks_ready, 1)
            nc.tensor.transpose(bank[4][0:E, 0:P], blocks_f[:], ident[:]).then_inc(blocks_turned, 1)
            pe.wait_ge(blocksT_ready, 1)
            mm(bank[5][:, 0:E], blocksT[:], upto[:], start=True, stop=True).then_inc(cum_mm, 1)
            pe.wait_ge(share_added, B)
            pe.wait_ge(table_ready, 1)
            pe.wait_ge(table_loaded, 16 * 3)
            pe.wait_ge(down_loaded, 16)

            expert_reg = [pe.alloc_register(f"expert{n}") for n in range(XG)]

            def load_expert(i, q, n, at):
                pe.reg_load(expert_reg[n], expert_row[0:1, bass.ds(i, 1)])

            def turn_rows(i, q, n, at):
                pe.wait_ge(xg_loaded[n], 16 * (q + 1))
                for k in range(KD):
                    last = nc.tensor.transpose(bank[n % 2][:, P * k:P * (k + 1)], xg[n][:, P * k:P * (k + 1)],
                                               ident[:])
                last.then_inc(xg_turned, 1)

            def up(i, q, n, at):
                e = pe.snap(expert_reg[n], min_val=0, max_val=E - 1)
                pe.wait_ge(xgT_ready, i + 1)
                for k in range(KD):
                    last = mm(bank[2 + n % 2][:, 0:2 * I], xgT[n % 2][:, P * k:P * (k + 1)],
                              gu_s[:, k, bass.ds(e, 1), :].rearrange("p a n -> p (a n)"), start=(k == 0),
                              stop=(k == KD - 1))
                last.then_inc(gu_mm, 1)

            def turn_hidden(i, q, n, at):
                pe.wait_ge(hs_ready, i + 1)
                nc.tensor.transpose(bank[4 + n % 2][:, 0:P], hs[n % 2], ident[:]).then_inc(hs_turned, 1)

            def down(i, q, n, at):
                e = pe.snap(expert_reg[n], min_val=0, max_val=E - 1)
                pe.wait_ge(hsT_ready, i + 1)
                if not (isinstance(i, int) and i < 2):
                    pe.wait_ge(y_ready, i - 1)
                mm(bank[6 + n % 2][:, 0:D], hsT[n % 2], dn_s[:, bass.ds(e, 1), :].rearrange("p a n -> p (a n)"),
                   start=True, stop=True).then_inc(y_mm, 1)

            run_blocks(pe, [turn_rows, up, load_expert, turn_hidden, down], [0, 1, 0, 2, 3])

        @block.scalar
        def _(act):
            a = nc.scalar.activation
            copy = nc.scalar.copy
            act.wait_ge(w_loaded, 16 * 5)
            a(sig_c[:], cT_s[:], ACT.Exp, scale=-1.0).then_inc(exp_c_ready, 1)

            def front(b, m, p):
                for k in range(KD):
                    act.wait_ge(h_turned, KD * b + k + 1)
                    copy(hT[:, k, :], bank[k][:]).then_inc(hT_ready, 1)
                for c in range(KD):
                    act.wait_ge(kt_mm, KD * b + c + 1)
                    copy(KT[:, c, :], bank[2 + c][:]).then_inc(KT_ready, 1)
                for c in range(2):
                    act.wait_ge(v_mm, 2 * b + c + 1)
                    copy(V[:, 2 * c:2 * c + 2, :].rearrange("p a d -> p (a d)"), bank[2 + c][:]).then_inc(V_ready, 1)

            def share(b, c):
                act.wait_ge(share_mm, KI * b + c + 1)
                a(th[:], bank[2][:], ACT.Tanh, scale=0.5).then_inc(tanh_ready, 1)

            def attention(b, m, p, late, more):
                def exps(i):
                    keys = P * (i + 1)
                    act.wait_ge(max_ready, NT * b + i + 1)
                    if i >= 2:
                        act.wait_ge(probs_turned, NT * b + i - 1)
                    a(probs[i % 2][:, 0:keys], bank[4 + i % 2][:, 0:keys], ACT.Exp, bias=negmax[:, i:i + 1],
                      accum_out=rowsum[:, i:i + 1]).then_inc(probs_ready, 1)

                def copy_turned(i):
                    act.wait_ge(probs_turned, NT * b + i + 1)
                    if i >= 2:
                        act.wait_ge(attended, NT * b + i - 1)
                    copy(pT_s[i % 2][:, 0:P * (i + 1)], bank[6][:, 0:P * (i + 1)]).then_inc(pT_ready, 1)

                exps(0)
                exps(1)
                if late:
                    share(b - 1, 0)
                copy_turned(0)
                exps(2)
                if late:
                    share(b - 1, 1)
                copy_turned(1)
                exps(3)
                copy_turned(2)
                copy_turned(3)
                if more:
                    front(b + 1, None, 1 - p)
                for k in range(KD):
                    act.wait_ge(h2_turned, KD * b + k + 1)
                    copy(h2T[:, k, :], bank[k][:]).then_inc(h2T_ready, 1)
                act.wait_ge(logits_mm, b + 1)
                a(esig[:].rearrange("p t e -> p (t e)"), bank[7][:, 0:NT * E], ACT.Exp, scale=-1.0
                  ).then_inc(esig_ready, 1)

            run_batches(act, front, attention)
            share(B - 1, 0)
            share(B - 1, 1)

            def copy_rows(i, q, n, at):
                act.wait_ge(xg_turned, i + 1)
                if not (isinstance(i, int) and i < 2):
                    act.wait_ge(gu_mm, i - 1)
                copy(xgT[n % 2], bank[n % 2][:, 0:D]).then_inc(xgT_ready, 1)

            def silu(i, q, n, at):
                act.wait_ge(gu_mm, i + 1)
                if not (isinstance(i, int) and i < 2):
                    act.wait_ge(hs_ready, i - 1)
                a(sg[n % 2], bank[2 + n % 2][:, 0:I], ACT.Silu).then_inc(silu_ready, 1)

            def copy_hidden(i, q, n, at):
                act.wait_ge(hs_turned, i + 1)
                if not (isinstance(i, int) and i < 2):
                    act.wait_ge(y_mm, i - 1)
                copy(hsT[n % 2], bank[4 + n % 2][:, 0:P]).then_inc(hsT_ready, 1)

            run_blocks(act, [copy_rows, silu, copy_hidden], [0, 1, 2])

            def store(n, m, k):
                act.wait_ge(out_ready, n + 1)
                apart(act)
                store_tile(act, n)
            run_tiles(act, [store])

        @block.vector
        def _(dve):
            v = nc.vector
            dve.wait_ge(exp_c_ready, 1)
            link = chain(dve, silu_c_steps, 0)
            link(v.tensor_scalar(sig_c[:], sig_c[:], 1.0, None, ALU.add))
            link(v.reciprocal(sig_c[:], sig_c[:]))
            v.tensor_tensor(silu_c[:], sig_c[:], cT_s[:], ALU.mult).then_inc(silu_c_steps, 1)
            dve.wait_ge(mod_mm, 1)
            for c in range(NM // 512):
                last = v.tensor_copy(mod[:, 512 * c:512 * (c + 1)], bank[c][0:B, :])
            last.then_inc(mod_steps, 1)
            dve.wait_ge(mod_steps, 1)
            for n in (CA, CB):
                v.tensor_scalar(mod[:, D * n:D * (n + 1)], mod[:, D * n:D * (n + 1)], 1.0, None, ALU.add)
            gates = [(sign[:, j, :], mod[:, D * n:D * (n + 1)]) for j, n in enumerate((GA, GB))]
            for twice, gate in gates:
                last = v.tensor_scalar(twice, gate, 0.0, 2.0, ALU.is_ge, ALU.mult)
            last.then_inc(mod_steps, 1)
            dve.wait_ge(mod_steps, 2)
            for twice, gate in gates:
                last = v.scalar_tensor_tensor(out=gate, in0=twice, scalar=1.0, in1=gate, op0=ALU.subtract, op1=ALU.mult)
            last.then_inc(mod_steps, 1)
            dve.wait_ge(mod_steps, 3)
            for twice, gate in gates:
                last = v.tensor_scalar(gate, gate, MIN_GATE, None, ALU.max)
            last.then_inc(mod_steps, 1)
            dve.wait_ge(mod_steps, 4)
            for twice, gate in gates:
                last = v.scalar_tensor_tensor(out=gate, in0=twice, scalar=1.0, in1=gate, op0=ALU.subtract, op1=ALU.mult)
            last.then_inc(mod_ready, 1)
            dve.wait_ge(consts_ready, 1)

            NORM_STEPS = 5 + 4 * NEWTON + NT

            def normalise(b, steps, scale, shift, dst, ready):
                link = chain(dve, steps, NORM_STEPS * b)
                for t in range(NT):
                    last = v.bn_stats(st[:, t, :], tile_of(xs, b, t))
                link(last)
                apart(dve)
                for t in range(NT):
                    last = v.bn_aggr(mv[:, t, :], st[:, t, :])
                link(last)
                link(v.tensor_scalar(rs_v[:], mv[:, :, 1], LN_EPS, None, ALU.add))
                v.tensor_scalar(rs_i[:], rs_v[:].bitcast(I32), 1, None, ALU.logical_shift_right
                                ).then_inc(steps, 1)
                link.done[0] += 1
                dve.wait_ge(steps, NORM_STEPS * b + link.done[0])
                y = rs_y
                last = v.tensor_scalar(y[:].bitcast(I32), rs_i[:], -1.0, float(RSQRT_SEED), ALU.mult, ALU.add)
                for n in range(NEWTON):
                    link(last)
                    link(v.tensor_tensor(rs_a[:], y[:], y[:], ALU.mult))
                    link(v.tensor_tensor(rs_b[:], rs_a[:], rs_v[:], ALU.mult))
                    link(v.tensor_scalar(rs_c[:], rs_b[:], -0.5, 1.5, ALU.mult, ALU.add))
                    last = v.tensor_tensor(y[:], y[:], rs_c[:], ALU.mult)
                link(last)
                for t in range(NT):
                    v.scalar_tensor_tensor(out=u[t % 2], in0=tile_of(xs, b, t), scalar=mv[:, t, 0:1], in1=scale,
                                           op0=ALU.subtract, op1=ALU.mult).then_inc(steps, 1)
                    link.done[0] += 1
                    dve.wait_ge(steps, NORM_STEPS * b + link.done[0])
                    v.scalar_tensor_tensor(out=dst(t), in0=u[t % 2], scalar=y[:, t:t + 1], in1=shift,
                                           op0=ALU.mult, op1=ALU.add).then_inc(ready, 1)
                assert link.done[0] == NORM_STEPS, link.done

            def front(b, m, p):
                dve.wait_ge(x_loaded[p], 16 * (m + 1))
                apart(dve)
                dve.wait_ge(bc_loaded[p], 16 * (m + 1))
                apart(dve)
                normalise(b, front_steps, bc[p][:, CA, :], bc[p][:, SA, :], lambda t: h[p][:, t, :], h_ready)

            CHOOSE = 13

            def choose_groups(b):
                link = chain(dve, choose_steps, CHOOSE * b)
                dve.wait_ge(esig_ready, b + 1)
                link(v.tensor_scalar(esig[:], esig[:], 1.0, None, ALU.add))
                link(v.reciprocal(scores[:], esig[:]))
                link(v.tensor_tensor(sfc[:], scores[:], bias_s[:].to_broadcast([P, NT, E]), ALU.add))
                link(v.tensor_reduce(gs[:], sfc[:].rearrange("p t (g e) -> p t g e", e=EG), AX.X, ALU.max))
                for t in range(NT):
                    other = gs[:, t, :].rearrange("p (a g) -> p a g", a=1).to_broadcast([P, N_GROUP, N_GROUP])
                    this = gs[:, t, :].rearrange("p (g a) -> p g a", a=1).to_broadcast([P, N_GROUP, N_GROUP])
                    v.tensor_tensor(cgt[:, t], other, this, ALU.is_gt)
                    last = v.tensor_tensor(ceq[:, t], other, this, ALU.is_equal)
                link(last)
                for t in range(NT):
                    last = v.tensor_tensor(ceq[:, t], ceq[:, t], before[:], ALU.mult)
                link(last)
                link(v.tensor_tensor(cgt, cgt, ceq, ALU.add))
                link(v.tensor_reduce(rank[:], cgt, AX.X, ALU.add))
                link(v.tensor_scalar(rank[:], rank[:], float(TOPK_GROUP), None, ALU.is_lt))
                for t in range(NT):
                    last = v.tensor_tensor(masked[:, t, :].rearrange("p (g e) -> p g e", e=EG),
                                           sfc[:, t, :].rearrange("p (g e) -> p g e", e=EG),
                                           rank[:, t, :].rearrange("p (g a) -> p g a", a=1).to_broadcast([P, N_GROUP, EG]),
                                           ALU.mult)
                link(last)
                return link

            def choose_experts(b, p, link):
                apart(dve)
                for t in range(NT):
                    last = v.max(m8[:, t, :], masked[:, t, :])
                link(last)
                apart(dve)
                for t in range(NT):
                    last = v.max_index(i8[:, t, :], m8[:, t, :], masked[:, t, :])
                link(last)
                link(v.tensor_copy(idx[:], i8[:, :, 0:TOP_K]))
                assert link.done[0] == CHOOSE, link.done
                for t in range(NT):
                    last = v.tensor_tensor(eq[:, t], idx[:, t, :].rearrange("p (j a) -> p j a", a=1).to_broadcast([P, TOP_K, E]),
                                           experts_iota[:].rearrange("p (a e) -> p a e", a=1).to_broadcast([P, TOP_K, E]),
                                           ALU.is_equal)
                last.then_inc(eq_ready, 1)
                dve.wait_ge(eq_ready, b + 1)
                with nc.allow_low_precision(reason="whole numbers, at most one of them not 0"):
                    v.tensor_reduce(sel[:], eq[:].rearrange("p t j e -> p t e j"), AX.X, ALU.add
                                    ).then_inc(sel_ready, 1)
                v.tensor_copy(rows[p][:, :, D:D + TOP_K], idx[:])
                v.tensor_copy(rows[p][:, :, D + TOP_K:D + 2 * TOP_K], dest0[:])

            PLACE = 7

            def place(b, p):
                link = chain(dve, place_steps, PLACE * b)
                for t in range(NT):
                    last = v.tensor_tensor(pr[:, t], eq[:, t],
                                           scores[:, t, :].rearrange("p (a e) -> p a e", a=1).to_broadcast([P, TOP_K, E]), ALU.mult)
                link(last)
                link(v.tensor_reduce(raw[:], pr[:], AX.X, ALU.add))
                link(v.tensor_reduce(tsum[:], raw[:], AX.X, ALU.add))
                link(v.tensor_scalar(tsum[:], tsum[:], 1e-20, None, ALU.add))
                link(v.reciprocal(tsum[:], tsum[:]))
                for t in range(NT):
                    v.tensor_scalar(rows[p][:, t, D + 2 * TOP_K:ROW], raw[:, t, :], tsum[:, t:t + 1], ROUTE_SCALE,
                                    ALU.mult, ALU.mult)
                dve.wait_ge(rank_mm, b + 1)
                for t in range(NT):
                    last = v.tensor_tensor(sfc[:, t, :], bank[2][:, E * t:E * (t + 1)], base[:], ALU.add)
                link(last)
                v.tensor_tensor(base[:], base[:], bank[3][:, 0:E], ALU.add).then_inc(rank_read, 1)
                for t in range(NT):
                    last = v.tensor_tensor(pr[:, t], eq[:, t],
                                           sfc[:, t, :].rearrange("p (a e) -> p a e", a=1).to_broadcast([P, TOP_K, E]), ALU.mult)
                link(last)
                assert link.done[0] == PLACE, link.done
                v.tensor_scalar(dest0[:], dest0[:], float(S * TOP_K), None, ALU.add)
                with nc.allow_low_precision(reason="whole numbers, at most one of them not 0"):
                    v.tensor_reduce(pos[p][:], pr[:], AX.X, ALU.add).then_inc(pos_ready, 1)

            def share(b, c):
                dve.wait_ge(tanh_ready, KI * b + c + 1)
                v.scalar_tensor_tensor(out=th[:], in0=th[:], scalar=1.0, in1=bank[2][:], op0=ALU.add, op1=ALU.mult
                                       ).then_inc(share_steps, 1)
                dve.wait_ge(share_steps, (KI + NT) * b + c + 1)
                v.scalar_tensor_tensor(out=sh[:, c, :], in0=th[:], scalar=0.5, in1=bank[3][:], op0=ALU.mult,
                                       op1=ALU.mult).then_inc(share_hidden, 1)

            def add_share(b):
                dve.wait_ge(share_down, b + 1)
                gb = tile_of(gb_all, 0, b)
                for t in range(NT):
                    half = th[:, D * (t % 2):D * (t % 2 + 1)]
                    v.tensor_tensor(half, bank[t // 2][:, D * (t % 2):D * (t % 2 + 1)], gb, ALU.mult
                                    ).then_inc(share_steps, 1)
                    dve.wait_ge(share_steps, (KI + NT) * b + KI + t + 1)
                    last = v.tensor_tensor(tile_of(xs, b, t), tile_of(xs, b, t), half, ALU.add)
                last.then_inc(share_added, 1)

            def attention(b, m, p, late, more):
                def row_max(i):
                    dve.wait_ge(scored, NT * b + i + 1)
                    v.tensor_reduce(negmax[:, i:i + 1], bank[4 + i % 2][:, 0:P * (i + 1)], AX.X, ALU.max, negate=True
                                    ).then_inc(max_ready, 1)

                steps = chain(dve, attend_steps, 2 * NT * b)

                def output(i):
                    dve.wait_ge(attended, NT * b + i + 1)
                    steps(v.reciprocal(rinv[:, i:i + 1], rowsum[:, i:i + 1]))
                    v.scalar_tensor_tensor(out=t1, in0=bank[7][:, 0:D], scalar=rinv[:, i:i + 1], in1=h[p][:, i, :],
                                           op0=ALU.mult, op1=ALU.add).then_inc(o_scaled, 1)
                    dve.wait_ge(o_scaled, NT * b + i + 1)
                    steps(v.tensor_tensor(t2[i % 2], t1, bc[p][:, GA, :], ALU.mult))
                    v.tensor_tensor(tile_of(xs, b, i), tile_of(xs, b, i), t2[i % 2], ALU.add).then_inc(x2_ready, 1)

                row_max(0)
                row_max(1)
                if late:
                    link = choose_groups(b - 1)
                    share(b - 1, 0)
                    choose_experts(b - 1, 1 - p, link)
                row_max(2)
                output(0)
                if late:
                    share(b - 1, 1)
                if more:
                    front(b + 1, m + 1 if p == 1 else m, 1 - p)
                row_max(3)
                output(1)
                if late:
                    add_share(b - 1)
                output(2)
                if late:
                    place(b - 1, 1 - p)
                output(3)
                dve.wait_ge(x2_ready, NT * b + NT)
                apart(dve)
                if late:
                    dve.wait_ge(rows_free, b)
                    apart(dve)
                normalise(b, norm2_steps, bc[p][:, CB, :], bc[p][:, SB, :], lambda t: rows[p][:, t, 0:D], h2_ready)

            dve.wait_ge(gb_loaded, 16)
            run_batches(dve, front, attention)
            link = choose_groups(B - 1)
            share(B - 1, 0)
            choose_experts(B - 1, (B - 1) % 2, link)
            share(B - 1, 1)
            place(B - 1, (B - 1) % 2)

            link = chain(dve, table_steps, 0)
            dve.wait_ge(rank_read, B)
            v.tensor_copy(base_i[:], base[:])
            link(v.tensor_tensor(cum[:], base[:], area[:], ALU.subtract))
            link(v.tensor_scalar(blocks_i[:], cum[:], float(P - 1), None, ALU.add))
            link(v.tensor_scalar(blocks_i[:], blocks_i[:], P.bit_length() - 1, None, ALU.logical_shift_right))
            v.tensor_copy(blocks_f[:], blocks_i[:]).then_inc(blocks_ready, 1)
            dve.wait_ge(blocks_turned, 1)
            v.tensor_copy(blocksT[:], bank[4][0:E, 0:P]).then_inc(blocksT_ready, 1)
            dve.wait_ge(cum_mm, 1)
            link(v.tensor_copy(cum[:], bank[5][:, 0:E]))
            link(v.tensor_tensor(cum_ex[:], cum[:], blocks_f[:], ALU.subtract))
            for n in range(NH):
                link(v.tensor_scalar(hit[:], cum[:], block_no[:, n:n + 1], None, ALU.is_le))
                link(v.tensor_reduce(e_f[:, n:n + 1], hit[:], AX.X, ALU.add))
                link(v.scalar_tensor_tensor(out=hit[:], in0=experts_iota[:], scalar=e_f[:, n:n + 1], in1=cum_ex[:],
                                            op0=ALU.is_equal, op1=ALU.mult))
                link(v.tensor_reduce(skipped[:, n:n + 1], hit[:], AX.X, ALU.add))
            v.tensor_scalar(table_e[:], e_f[:], float(E - 1), None, ALU.min)
            v.tensor_scalar(table_f[:], e_f[:], float(E - 1), None, ALU.min)
            link(v.tensor_scalar(valid[:], e_f[:], float(E), float(P), ALU.is_lt, ALU.mult))
            link(v.tensor_tensor(r1[:], block_no[:], skipped[:], ALU.subtract))
            link(v.tensor_tensor(r2[:], r1[:], valid[:], ALU.mult))
            v.scalar_tensor_tensor(out=table_r[:], in0=e_f[:], scalar=float(CAP), in1=r2[:], op0=ALU.mult, op1=ALU.add
                                   ).then_inc(table_ready, 1)
            add_share(B - 1)
            dve.wait_ge(table_loaded, 16 * 3)

            def find_dest(i, q, n, at):
                dve.wait_ge(xg_loaded[n], 16 * (q + 1))
                apart(dve)
                v.scalar_tensor_tensor(out=match[:, n % 2],
                                       in0=xg[n][:, D:D + TOP_K].rearrange("p (a j) -> p a j", a=1)
                                       .to_broadcast([P, 2, TOP_K]), scalar=expert_bc[:, bass.ds(i, 1)],
                                       in1=xg[n][:, D + TOP_K:ROW].rearrange("p (a j) -> p a j", a=2),
                                       op0=ALU.is_equal, op1=ALU.mult).then_inc(dest_steps, 1)
                dve.wait_ge(dest_steps, 2 * i + 1)
                v.tensor_reduce(found[:, n, :], match[:, n % 2], AX.X, ALU.add).then_inc(dest_steps, 1)
                dve.wait_ge(dest_steps, 2 * i + 2)
                if not (isinstance(i, int) and i < XG):
                    dve.wait_ge(y_scattered[n], 16 * q)
                v.tensor_scalar(dest[n][:], found[:, n, 0:1], -1.0, None, ALU.add).then_inc(dest_ready, 1)

            def hidden(i, q, n, at):
                dve.wait_ge(silu_ready, i + 1)
                if not (isinstance(i, int) and i < 2):
                    dve.wait_ge(hs_turned, i - 1)
                v.tensor_tensor(hs[n % 2], sg[n % 2], bank[2 + n % 2][:, I:2 * I], ALU.mult).then_inc(hs_ready, 1)

            def copy_out(i, q, n, at):
                dve.wait_ge(y_mm, i + 1)
                v.tensor_scalar(yb[n], bank[6 + n % 2][:, 0:D], found[:, n, 1:2], None, ALU.mult
                                ).then_inc(y_ready, 1)

            run_blocks(dve, [find_dest, hidden, copy_out], [1, 1, 3])

            def halve(n, m, k):
                dve.wait_ge(y_loaded[k], 16 * (m + 1))
                v.tensor_tensor(y3[k], yt[k][:, 0:3 * D], yt[k][:, 3 * D:6 * D], ALU.add).then_inc(halved, 1)

            def two_of_three(n, m, k):
                dve.wait_ge(halved, n + 1)
                v.tensor_tensor(y1[k], y3[k][:, 0:D], y3[k][:, D:2 * D], ALU.add).then_inc(added, 1)

            run_tiles(dve, [halve, two_of_three])


def kernel(**inputs):
    import numpy as np
    import concourse.bacc as bacc
    from concourse import mybir as mb
    from concourse.bass_utils import run_bass_kernel_spmd as run

    f = {k: np.asarray(a) for k, a in inputs.items()}
    arrays = {
        "x": f["L0_attn_x"], "wT": f["L0_attn_W"].T, "gateT": f["L0_ffn_gate_weight"].T,
        "bias": f["L0_ffn_e_score_correction_bias"],
        "guT": f["L0_ffn_experts_gate_up"].transpose(0, 2, 1), "dnT": f["L0_ffn_experts_down"].transpose(0, 2, 1),
        "sguT": np.concatenate([f["L0_ffn_shared_gate_w"], f["L0_ffn_shared_up_w"]], axis=0).T,
        "sdnT": f["L0_ffn_shared_down_w"].T,
        "cT": f["L0_c"].T, "wmod": f["L0_wmod"],
    }
    arrays = {k: np.ascontiguousarray(a) for k, a in arrays.items()}
    nc = bacc.Bacc("TRN2", target_bir_lowering=False, num_devices=1)
    args = [nc.dram_tensor(k, a.shape, mb.dt.from_np(a.dtype), kind="ExternalInput").ap() for k, a in arrays.items()]
    out = nc.dram_tensor("out", f["L0_attn_x"].shape, mb.dt.float32, kind="ExternalOutput").ap()
    build_adaln_block(nc, *args, out)
    r = run(nc, [arrays], core_ids=[0])
    return r.results[0]["out"]
```

```python
from contextlib import ExitStack

import concourse.bass as bass
from concourse import mybir

P = 128
ALU = mybir.AluOpType
ACT = mybir.ActivationFunctionType
AX = mybir.AxisListType
F32 = mybir.dt.float32
BF16 = mybir.dt.bfloat16
I32 = mybir.dt.int32
U32 = mybir.dt.uint32

LN_EPS = 1e-5
MIN_GATE = 0.25
MASKED = -1e30
N_GROUP, TOPK_GROUP, TOP_K, ROUTE_SCALE = 8, 4, 6, 2.5
SA, CA, GA, SB, CB, GB = range(6)
RSQRT_SEED = 0x5F3759DF
NEWTON = 3
XG = 8
YT = 8


def build_adaln_block(nc, x, wT, gateT, bias, guT, dnT, sguT, sdnT, cT, wmod, out):
    B, S, D = x.shape
    E = gateT.shape[1]
    I = dnT.shape[1]
    SI = sdnT.shape[0]
    KD = D // P
    KI = SI // P
    NT = S // P
    T = B * S
    NM = 6 * D
    EG = E // N_GROUP
    CAP = T + P
    ROWS = E * CAP + P
    ROW = D + 3 * TOP_K
    BLOCKS = T * TOP_K // P + E
    NH = -(-BLOCKS // P)
    SURE = ((B - 1) * S * TOP_K - E * (P - 1)) // P // XG * XG
    SLOTS = 2 * E + 1
    assert NH == 2 and P <= SURE

    with ExitStack() as ctx:
        def sb(name, shape, dt=F32):
            return ctx.enter_context(nc.sbuf_tensor(name, shape, dt))

        def sem(name):
            return ctx.enter_context(nc.semaphore(name))

        xs = sb("xs", [P, B * NT, D])
        gu_s = sb("gu_s", [P, KD, E, 2 * I])
        dn_s = sb("dn_s", [P, E, D])
        sgu_s = sb("sgu_s", [P, KD, 2 * SI])
        sdn_s = sb("sdn_s", [P, KI, D])
        gb_all = sb("gb_all", [P, B, D])
        ident = sb("ident", [P, P])
        ident_bf = sb("ident_bf", [P, P], BF16)
        causal = sb("causal", [P, P], BF16)
        earlier = sb("earlier", [P, P], BF16)
        ones_bf = sb("ones_bf", [P, P], BF16)
        before = sb("before", [P, N_GROUP, N_GROUP])
        experts_iota = sb("experts_iota", [P, E])
        area = sb("area", [P, E])
        block_no = sb("block_no", [P, NH])
        base = sb("base", [P, E])
        dest0 = sb("dest_of_token", [P, NT, TOP_K])
        taken = [0]

        def early(free, parts=P):
            view = dn_s[:].rearrange("p e d -> p (e d)")[0:parts, taken[0]:taken[0] + free]
            taken[0] += free
            return view

        wT_s = early(KD * 2 * D).rearrange("p (k n) -> p k n", k=KD)
        mod = early(NM, B)
        sign = early(2 * D, B).rearrange("p (j d) -> p j d", j=2)
        u = [early(D) for t in range(NT)]
        t1 = early(D)
        t2 = [early(D) for n in (0, 1)]
        probs = [early(S) for p in (0, 1)]
        pT_s = [early(NT * P) for p in (0, 1)]
        gateT_s = sb("gateT_s", [P, KD, E])
        bias_s = sb("bias_s", [P, 1, E])
        cT_s = sb("cT_s", [P, KD, B])
        silu_c = sb("silu_c", [P, KD, B])
        sig_c = sb("sig_c", [P, KD, B])
        bc = [sb(f"bc{p}", [P, 5, D]) for p in (0, 1)]
        pad = sb("pad", [P, ROW])

        st = sb("st", [P, 2 * NT, 6])
        mv = sb("mv", [P, 2 * NT, 2])
        rs_v, rs_y, rs_a, rs_b = (sb(f"rs_{n}", [P, 2 * NT]) for n in "vyab")
        rs_i = sb("rs_i", [P, 2 * NT], I32)
        h = [sb(f"h{p}", [P, NT, D]) for p in (0, 1)]
        rows = [sb(f"rows{p}", [P, NT, ROW]) for p in (0, 1)]
        hT = sb("hT", [P, KD, S])
        KT = sb("KT", [P, KD, S])
        V = sb("V", [P, NT, D])
        h2T = sb("h2T", [P, KD, S])
        negmax = sb("negmax", [P, NT])
        rowsum = sb("rowsum", [P, NT])
        rinv = sb("rinv", [P, NT])
        th = sb("th", [P, S])
        esigT = th[0:E, :]
        sh = sb("sh", [P, KI, S])
        esig = sb("esig", [P, NT, E])
        scores = sb("scores", [P, NT, E])
        sfc = sb("sfc", [P, NT, E])
        gs = sb("gs", [P, NT, N_GROUP])
        eq = sb("eq", [P, NT, TOP_K, E])
        pr = sb("pr", [P, NT, TOP_K, E])
        cgt = eq[:].rearrange("p t j e -> p (t j e)")[:, 0:NT * N_GROUP ** 2].rearrange(
            "p (t g o) -> p t g o", t=NT, g=N_GROUP)
        ceq = pr[:].rearrange("p t j e -> p (t j e)")[:, 0:NT * N_GROUP ** 2].rearrange(
            "p (t g o) -> p t g o", t=NT, g=N_GROUP)
        rank = sb("rank", [P, NT, N_GROUP])
        masked = sb("masked", [P, NT, E])
        m8 = sb("m8", [P, NT, 8])
        i8 = sb("i8", [P, NT, 8], U32)
        idx = sb("idx", [P, NT, TOP_K])
        sel = sb("sel", [P, NT, E], BF16)
        pos = [sb(f"pos{p}", [P, NT, TOP_K], I32) for p in (0, 1)]
        raw = sb("raw", [P, NT, TOP_K])
        tsum = sb("tsum", [P, NT])

        slot_no = sb("slot_no", [P, SLOTS])
        expert_of = sb("expert_of", [P, SLOTS])
        first = sb("first", [P, SLOTS])
        cum = sb("cum", [P, 2 * E])
        cum_ex = sb("cum_ex", [P, E])
        rows_of = sb("rows_of", [P, E])
        blocks_i = sb("blocks_i", [P, E], I32)
        full = sb("full", [P, E])
        blocks_f = sb("blocks_f", [P, E])
        rest = sb("rest", [P, E])
        running = [sb(f"running{p}", [P, E]) for p in (0, 1)]
        hit = sb("hit", [P, SLOTS])
        hit_first = sb("hit_first", [P, SLOTS])
        slot = sb("slot", [P, 1])
        row_f = sb("row_f", [P, 1])
        expert_f = sb("expert_f", [P, 1])
        table_f = sb("table_f", [P, NH + 1])
        table_e = sb("table_e", [P, NH + 1], I32)
        table_r = sb("table_r", [P, NH + 1], I32)
        base_i = sb("base_i", [P, E], I32)

        expert_row = bc[0][0:1, 0, 0:NH * P].bitcast(I32)
        start_row = bc[0][0:1, 1, 0:NH * P].bitcast(I32)
        expert_bc = bc[0][:, 2, 0:NH * P]

        hT_row, KT_row = (buf[:].rearrange("p k s -> p (k s)") for buf in (hT, KT))
        xg = [rows[0][:, n, :] for n in range(NT)] + [hT_row[:, ROW * n:ROW * (n + 1)] for n in range(3)] + \
             [KT_row[:, 0:ROW]]
        yb = [h[n // NT][:, n % NT, :] for n in range(XG)]
        xgT = [V[:, n, :] for n in (0, 1)]
        sg = [h2T[:, 0, P * n:P * (n + 1)] for n in (0, 1)]
        hs = [h2T[:, 0, P * (n + 2):P * (n + 3)] for n in (0, 1)]
        hsT = [h2T[:, 1, P * n:P * (n + 1)] for n in (0, 1)]
        found = sb("found", [P, XG, 2])
        match = sb("match", [P, 2, 2, TOP_K])
        dest = [sb(f"place{n}", [P, 1], I32) for n in range(XG)]

        wmod_s = gu_s[:, 0, 0:KD * NM // (2 * I), :].rearrange("p a n -> p (a n)").rearrange(
            "p (k n) -> p k n", k=KD)

        mod_dram = nc.dram_tensor("mod_dram", [B, NM], F32)
        sorted_dram = nc.dram_tensor("sorted_dram", [ROWS, ROW], F32)
        y_dram = nc.dram_tensor("y_dram", [T * TOP_K, D], F32)
        expert_dram = nc.dram_tensor("expert_dram", [NH * P], I32)
        start_dram = nc.dram_tensor("start_dram", [NH * P], I32)
        expert_f_dram = nc.dram_tensor("expert_f_dram", [NH * P], F32)

        bank = [ctx.enter_context(nc.psum_tensor(f"bank{i}", [P, 512], F32)) for i in range(8)]

        mod_bank = [bank[0], bank[6], bank[7]]

        w_loaded = sem("w_loaded")
        experts_loaded = sem("experts_loaded")
        down_loaded = sem("down_loaded")
        c_loaded = sem("c_loaded")
        wmod_first = sem("wmod_first")
        wmod_rest = sem("wmod_rest")
        x_loaded = [sem("x_loaded0"), sem("x_loaded1")]
        x_rest_loaded = sem("x_rest_loaded")
        mod_first_ready = sem("mod_first_ready")
        bc_first = [sem("bc_first0"), sem("bc_first1")]
        mod_stored = sem("mod_stored")
        bc_loaded = [sem("bc_loaded0"), sem("bc_loaded1")]
        gb_loaded = sem("gb_loaded")
        pool_const = sem("pool_const")
        consts_ready = sem("consts_ready")
        exp_c_ready = sem("exp_c_ready")
        silu_c_steps = sem("silu_c_steps")
        mod_mm = sem("mod_mm")
        mod_steps = sem("mod_steps")
        mod_ready = sem("mod_ready")
        sums_ahead = sem("sums_ahead")
        stat_steps = sem("stat_steps")
        attend_steps = sem("attend_steps")
        choose_steps = sem("choose_steps")
        place_steps = sem("place_steps")
        rank_steps = sem("rank_steps")
        share_steps = sem("share_steps")
        front_scaled = sem("front_scaled")
        norm2_scaled = sem("norm2_scaled")
        front_normal = sem("front_normal")
        norm2_normal = sem("norm2_normal")
        h_ready = sem("h_ready")
        h_turned = sem("h_turned")
        hT_ready = sem("hT_ready")
        kt_mm = sem("kt_mm")
        KT_ready = sem("KT_ready")
        v_mm = sem("v_mm")
        V_ready = sem("V_ready")
        scored = sem("scored")
        max_ready = sem("max_ready")
        probs_ready = sem("probs_ready")
        probs_turned = sem("probs_turned")
        pT_ready = sem("pT_ready")
        attended = sem("attended")
        o_scaled = sem("o_scaled")
        x2_ready = sem("x2_ready")
        h2_ready = sem("h2_ready")
        h2_turned = sem("h2_turned")
        h2T_ready = sem("h2T_ready")
        logits_mm = sem("logits_mm")
        esigT_ready = sem("esigT_ready")
        esig_turned = sem("esig_turned")
        eq_ready = sem("eq_ready")
        sel_ready = sem("sel_ready")
        rank_mm = sem("rank_mm")
        rank_read = sem("rank_read")
        pos_ready = sem("pos_ready")
        scattered = [sem("scattered0"), sem("scattered1")]
        share_mm = sem("share_mm")
        tanh_ready = sem("tanh_ready")
        share_hidden = sem("share_hidden")
        share_down = sem("share_down")
        share_gated = sem("share_gated")
        share_added = sem("share_added")
        table_steps = sem("table_steps")
        table_ready = sem("table_ready")
        table_stored = sem("table_stored")
        table_loaded = sem("table_loaded")
        base_ready = sem("base_ready")
        padded = sem("padded")
        xg_loaded = [sem(f"xg_loaded{n}") for n in range(XG)]
        xg_turned = sem("xg_turned")
        xgT_ready = sem("xgT_ready")
        gu_mm = sem("gu_mm")
        silu_ready = sem("silu_ready")
        hs_ready = sem("hs_ready")
        hs_turned = sem("hs_turned")
        hsT_ready = sem("hsT_ready")
        y_mm = sem("y_mm")
        dest_steps = sem("dest_steps")
        dest_ready = sem("dest_ready")
        y_ready = sem("y_ready")
        y_scattered = [sem(f"y_scattered{n}") for n in range(XG)]
        y_loaded = [sem(f"y_loaded{k}") for k in range(YT)]
        halved = sem("halved")
        added = sem("added")
        summed = sem("summed")
        gated = sem("gated")
        out_ready = sem("out_ready")
        out_stored = sem("out_stored")
        waits_apart = sem("waits_apart")

        def apart(eng):
            eng.sem_inc(waits_apart, 1)

        def run_batches(eng, front, attention):
            front(0, 0, 0)
            attention(0, 0, 0, False, True)
            attention(1, 0, 1, True, True)
            with eng.Fori(1, B // 2 - 1) as m:
                attention(2 * m, m, 0, True, True)
                attention(2 * m + 1, m, 1, True, True)
            attention(B - 2, B // 2 - 1, 0, True, True)
            attention(B - 1, B // 2 - 1, 1, True, False)

        def attended_in(i):
            return bank[7 if i < NT - 1 else 5]

        def turned_in(i):
            return bank[6 if i < NT - 1 else 4]

        def first_slot(b):
            return 0 if isinstance(b, int) and b == 0 else NT

        def chain(eng, steps, base):
            done = [0]

            def link(ins):
                done[0] += 1
                ins.then_inc(steps, 1)
                eng.wait_ge(steps, base + done[0])
            link.done = done
            return link

        def run_blocks(eng, stages, skew, begin_turn=None, later=None):
            deep = max(skew)

            def one(r, q, k):
                for stage, s in zip(stages, skew):
                    if isinstance(r, int) and not 0 <= r - s < BLOCKS:
                        continue
                    stage(r - s, q + (k - s) // XG, (k - s) % XG, k - s)
            begin_turn = begin_turn or (lambda q: None)
            begin_turn(0)
            for r in range(XG):
                one(r, 0, r)
            for turns in ((1, SURE // XG), (SURE // XG, BLOCKS // XG)):
                if turns[0] > 1 and later:
                    later()
                with eng.Fori(*turns) as q:
                    begin_turn(q)
                    for k in range(XG):
                        one(XG * q + k, q, k)
            if deep:
                begin_turn(BLOCKS // XG)
            for r in range(BLOCKS, BLOCKS + deep):
                one(r, BLOCKS // XG, r - BLOCKS)

        def tile_of(buf, b, i):
            return buf[:, bass.ds(NT * b + i, 1), :].rearrange("p a d -> p (a d)")

        yt_place = gu_s[:].rearrange("p k e n -> p (k e n)")
        yt = [yt_place[:, TOP_K * D * k:TOP_K * D * (k + 1)] for k in range(YT)]
        y3 = [t[:, 0:3 * D] for t in yt]
        y1 = [t[:, 3 * D:4 * D] for t in yt]
        yg = [t[:, 4 * D:5 * D] for t in yt]

        def run_tiles(eng, stages):
            with eng.Fori(0, B * NT // YT) as m:
                for k in range(YT + len(stages) - 1):
                    for s, stage in enumerate(stages):
                        if 0 <= k - s < YT:
                            stage(YT * m + k - s, m, k - s)

        def load_outputs(eng, n, k):
            src = y_dram[bass.ds(n * (P * TOP_K), P * TOP_K), :].rearrange("(p j) d -> p (j d)", j=TOP_K)
            eng.dma_start(yt[k], src).then_inc(y_loaded[k], 16)

        def store_tile(eng, n):
            eng.dma_start(out.rearrange("b s d -> (b s) d")[bass.ds(n * P, P), :], tile_of(xs, 0, n)
                          ).then_inc(out_stored, 16)

        def store_table(eng, column, start, stop):
            place = P * min(column, NH - 1)
            for dst, src in ((expert_dram, table_e), (start_dram, table_r), (expert_f_dram, table_f)):
                eng.dma_start(dst[place + start:place + stop].rearrange("(p a) -> p a", a=1),
                              src[start:stop, column:column + 1]).then_inc(table_stored, 16)

        def load_table(eng, start, stop):
            for dst, src in ((start_row, start_dram), (expert_row, expert_dram)):
                eng.dma_start(dst[:, start:stop], src[start:stop].rearrange("(a n) -> a n", a=1)
                              ).then_inc(table_loaded, 16)
            eng.dma_start(expert_bc[:, start:stop], expert_f_dram[start:stop].partition_broadcast(P)
                          ).then_inc(table_loaded, 16)

        block = ctx.enter_context(nc.Block())

        @block.sync
        def _(sp):
            pieces = lambda a: a.rearrange("(k p) n -> p k n", p=P)
            sp.dma_start(cT_s[:], pieces(cT)).then_inc(c_loaded, 16)
            sp.dma_start(wmod_s[:, :, 0:2 * D], pieces(wmod)[:, :, 0:2 * D]).then_inc(wmod_first, 16)
            for b in range(2):
                sp.dma_start(xs[:, NT * b:NT * (b + 1), :],
                             x[b].rearrange("(t p) d -> p t d", p=P)).then_inc(x_loaded[b], 16)
            sp.dma_start(wT_s, pieces(wT)).then_inc(w_loaded, 16)
            sp.dma_start(wmod_s[:, :, 2 * D:], pieces(wmod)[:, :, 2 * D:]).then_inc(wmod_rest, 16)
            sp.dma_start(gateT_s[:], pieces(gateT)).then_inc(w_loaded, 16)
            sp.dma_start(bias_s[:, 0, :], bias.partition_broadcast(P)).then_inc(w_loaded, 16)
            sp.wait_ge(mod_first_ready, 1)
            sp.dma_start(mod_dram[:, 0:2 * D], mod[:, 0:2 * D]).then_inc(mod_stored, 16)
            sp.wait_ge(mod_stored, 16)
            for b in range(2):
                sp.dma_start(bc[b][:, 0:2, :].rearrange("p a d -> p (a d)"),
                             mod_dram[b, 0:2 * D].partition_broadcast(P)).then_inc(bc_first[b], 16)
            sp.wait_ge(mod_ready, 1)
            sp.dma_start(mod_dram[:, 2 * D:], mod[:, 2 * D:]).then_inc(mod_stored, 16)
            sp.wait_ge(mod_stored, 16 * 2)
            for b in range(2):
                sp.dma_start(bc[b][:, 2:, :].rearrange("p a d -> p (a d)"),
                             mod_dram[b, 2 * D:GB * D].partition_broadcast(P)).then_inc(bc_loaded[b], 16)
            for b in range(2, B):
                sp.dma_start(xs[:, NT * b:NT * (b + 1), :],
                             x[b].rearrange("(t p) d -> p t d", p=P)).then_inc(x_rest_loaded, 16)
            sp.dma_start(gb_all[:], mod_dram[:, GB * D:].partition_broadcast(P)).then_inc(gb_loaded, 16)
            sp.dma_start(sgu_s[:], sguT.rearrange("(k p) n -> p k n", p=P)).then_inc(experts_loaded, 16)
            sp.dma_start(sdn_s[:], sdnT.rearrange("(k p) n -> p k n", p=P)).then_inc(experts_loaded, 16)
            for k in range(KD):
                sp.dma_start(gu_s[:, k], guT[:, P * k:P * (k + 1), :].rearrange("e p n -> p e n")
                             ).then_inc(experts_loaded, 16)
            with sp.Fori(1, B // 2) as m:
                for p in (0, 1):
                    sp.wait_ge(h2_ready, NT * (2 * m + p - 1))
                    apart(sp)
                    sp.wait_ge(bc_loaded[p], 16 * m)
                    apart(sp)
                    sp.dma_start(bc[p][:].rearrange("p a d -> p (a d)"),
                                 mod_dram[bass.ds(2 * m + p, 1), 0:GB * D].rearrange("a n -> (a n)")
                                 .partition_broadcast(P)).then_inc(bc_loaded[p], 16)
            sp.wait_ge(h2_ready, NT * B)
            sp.dma_start(dn_s[:], dnT.rearrange("e p n -> p e n")).then_inc(down_loaded, 16)
            sp.wait_ge(table_ready, 1)
            store_table(sp, 0, 0, P)
            store_table(sp, 1, 0, SURE - P)
            sp.wait_ge(table_stored, 16 * 3 * 2)
            load_table(sp, 0, SURE)
            sp.dma_start(sorted_dram[E * CAP:E * CAP + P, :], pad[:]).then_inc(padded, 16)
            for p in (0, 1):
                sp.wait_ge(scattered[p], 16 * NT * TOP_K * ((B - p) // 2))
            sp.wait_ge(table_loaded, 16 * 3)

            first_row = {}

            def first_rows_of_turn(q):
                _, regs = nc.values_load_multi_w_load_instructions(
                    start_row[0:1, bass.ds(q * XG, XG)], (mybir.EngineType.SP,), min_val=0, max_val=ROWS - P)
                first_row.update(enumerate(regs))
                if isinstance(q, int) and q == 0:
                    return
                if pads_left:
                    sp.wait_ge(base_ready, 1)
                    _, last_rows = nc.values_load_multi_w_load_instructions(
                        base_i[0:1, bass.ds(2 * q - 2, 2)], (mybir.EngineType.SP,), min_val=0, max_val=ROWS - P)
                    for row in last_rows:
                        sp.dma_start(sorted_dram[bass.ds(row, P), :], pad[:]).then_inc(padded, 16)

            def load_rows(i, q, n, at):
                if not (isinstance(i, int) and i < XG):
                    sp.wait_ge(xg_turned, i - XG + 1)
                    apart(sp)
                    sp.wait_ge(dest_ready, i - XG + 1)
                    apart(sp)
                sp.dma_start(xg[n], sorted_dram[bass.ds(first_row[at], P), :]).then_inc(xg_loaded[n], 16)
            def last_rows_and_table():
                pads_left.clear()
                sp.wait_ge(table_ready, 2)
                store_table(sp, NH, SURE - P, P)
                sp.wait_ge(table_stored, 16 * 3 * 3)
                load_table(sp, SURE, NH * P)
                sp.wait_ge(padded, 16 * (E + 1))
                for p in (0, 1):
                    sp.wait_ge(scattered[p], 16 * NT * TOP_K * (B // 2))
                sp.wait_ge(table_loaded, 16 * 3 * 2)

            assert SURE // XG - 1 == E // 2
            pads_left = [True]
            run_blocks(sp, [load_rows], [0], first_rows_of_turn, last_rows_and_table)

            for n in range(XG):
                sp.wait_ge(y_scattered[n], 16 * (BLOCKS // XG))
            for k in range(YT):
                load_outputs(sp, k, k)
            with sp.Fori(1, B * NT // YT) as m:
                for k in range(YT):
                    sp.wait_ge(out_ready, YT * (m - 1) + k + 1)
                    apart(sp)
                    load_outputs(sp, YT * m + k, k)
            sp.wait_ge(out_stored, 16 * B * NT)

        @block.gpsimd
        def _(pool):
            g = nc.gpsimd
            iota = dict(allow_small_or_imprecise_dtypes=True)
            g.memset(ident[:], 0.0)
            g.memset(causal[:], 0.0)
            g.memset(before[:], 1.0)
            g.memset(earlier[:], 1.0)
            g.memset(ones_bf[:], 1.0)
            g.memset(first[:], float(E * CAP))
            g.memset(expert_of[:], 0.0).then_inc(pool_const, 1)
            g.iota(experts_iota[:], [[1, E]], base=0, channel_multiplier=0, **iota)
            g.iota(area[:], [[0, 1], [CAP, E]], base=0, channel_multiplier=0, **iota)
            g.iota(block_no[:], [[P, NH]], base=0, channel_multiplier=1, **iota)
            g.iota(dest0[:], [[P * TOP_K, NT], [1, TOP_K]], base=1, channel_multiplier=TOP_K, **iota)
            g.memset(pad[:], 0.0)
            pool.wait_ge(pool_const, 1)
            g.affine_select(out=ident[:], in_=ident[:], compare_op=ALU.not_equal, fill=1.0, base=0,
                            pattern=[[-1, P]], channel_multiplier=1)
            g.affine_select(out=causal[:], in_=causal[:], compare_op=ALU.is_ge, fill=MASKED, base=0,
                            pattern=[[-1, P]], channel_multiplier=1)
            g.affine_select(out=before[:], in_=before[:], compare_op=ALU.is_gt, fill=0.0, base=0,
                            pattern=[[1, N_GROUP], [-1, N_GROUP]], channel_multiplier=0)
            g.affine_select(out=earlier[:], in_=earlier[:], compare_op=ALU.is_gt, fill=0.0, base=0,
                            pattern=[[1, P]], channel_multiplier=-1)
            g.iota(slot_no[:], [[1, SLOTS]], base=0, channel_multiplier=0, **iota)
            g.iota(expert_of[:, 0:2 * E], [[0, 2], [1, E]], base=0, channel_multiplier=0, **iota
                   ).then_inc(pool_const, 1)
            pool.wait_ge(pool_const, 2)
            g.tensor_copy(base[:], area[:])
            g.tensor_copy(ident_bf[:], ident[:]).then_inc(consts_ready, 1)

            def front(b, m, p):
                for t in range(NT):
                    pool.wait_ge(front_normal, NT * b + t + 1)
                    apart(pool)
                    g.tensor_tensor(h[p][:, t, :], u[t], bc[p][:, SA, :], ALU.add).then_inc(h_ready, 1)

            def scatter(b, p, tiles, columns=range(TOP_K)):
                pool.wait_ge(pos_ready, b + 1)
                apart(pool)
                for t in tiles:
                    for j in columns:
                        g.indirect_dma_start(
                            out=sorted_dram[:, :], out_offset=bass.IndirectOffsetOnAxis(
                                ap=pos[p][:, t, j:j + 1].bitcast(U32), axis=0),
                            in_=rows[p][:, t, :], in_offset=None).then_inc(scattered[p], 16)

            def add_share(b):
                pool.wait_ge(share_gated, b + 1)
                apart(pool)
                for c in range(NT // 2):
                    two = xs[:, bass.ds(NT * b + 2 * c, 2), :]
                    last = g.tensor_tensor(two, two, sh[:, c, :].rearrange("p (a d) -> p a d", a=2), ALU.add)
                last.then_inc(share_added, 1)

            def attention(b, m, p, late, more):
                if more:
                    front(b + 1, None, 1 - p)
                if not (isinstance(b, int) and b < 2):
                    scatter(b - 2, p, LATER)
                if late:
                    add_share(b - 1)
                if not (isinstance(b, int) and b < 2):
                    pool.wait_ge(scattered[p], 16 * NT * TOP_K * m)
                    apart(pool)
                for t in range(NT):
                    pool.wait_ge(norm2_normal, NT * b + t + 1)
                    apart(pool)
                    g.tensor_tensor(rows[p][:, t, 0:D], u[t], bc[p][:, SB, :], ALU.add).then_inc(h2_ready, 1)
                if late:
                    scatter(b - 1, 1 - p, SOONER)

            SOONER, LATER = range(NT - 1), range(NT - 1, NT)
            run_batches(pool, front, attention)
            scatter(B - 2, B % 2, LATER)
            add_share(B - 1)
            scatter(B - 1, (B - 1) % 2, range(NT // 2))

            def scatter_outputs(i, q, n, at):
                pool.wait_ge(dest_ready, i + 1)
                apart(pool)
                pool.wait_ge(y_ready, i + 1)
                apart(pool)
                g.indirect_dma_start(
                    out=y_dram[:, :], out_offset=bass.IndirectOffsetOnAxis(ap=dest[n][:, 0:1].bitcast(U32), axis=0),
                    in_=yb[n], in_offset=None, bounds_check=T * TOP_K - 1, oob_is_err=False
                    ).then_inc(y_scattered[n], 16)
                if isinstance(i, int) and i < NT:
                    half = TOP_K // 2
                    scatter(B - 1, (B - 1) % 2, [NT // 2 + i // 2], range(half * (i % 2), half * (i % 2 + 1)))
            run_blocks(pool, [scatter_outputs], [0])

            def third(n, m, k):
                pool.wait_ge(added, n + 1)
                apart(pool)
                g.tensor_tensor(y1[k], y1[k], y3[k][:, 2 * D:3 * D], ALU.add).then_inc(summed, 1)

            def gate(n, m, k):
                pool.wait_ge(summed, n + 1)
                apart(pool)
                g.tensor_tensor(yg[k], y1[k], tile_of(gb_all, 0, YT // NT * m + k // NT), ALU.mult
                                ).then_inc(gated, 1)

            def add_x(n, m, k):
                pool.wait_ge(gated, n + 1)
                apart(pool)
                g.tensor_tensor(tile_of(xs, 0, n), tile_of(xs, 0, n), yg[k], ALU.add).then_inc(out_ready, 1)

            run_tiles(pool, [third, gate, add_x])

        @block.tensor
        def _(pe):
            mm = nc.tensor.matmul

            pe.wait_ge(silu_c_steps, 3)
            for c in range(NM // 512):
                if c < 2:
                    pe.wait_ge([wmod_first, wmod_rest][c], 16)
                for k in range(KD):
                    last = mm(mod_bank[c][0:B, :], silu_c[:, k, :], wmod_s[:, k, 512 * c:512 * (c + 1)],
                              start=(k == 0), stop=(k == KD - 1))
                last.then_inc(mod_mm, 1)
            pe.wait_ge(w_loaded, 16 * 3)
            pe.wait_ge(consts_ready, 1)

            def front(b, m, p):
                pe.wait_ge(h_ready, NT * b + NT)
                if not (isinstance(b, int) and b < 2):
                    pe.wait_ge(share_gated, b - 1)
                for k in range(KD):
                    for t in range(NT):
                        last = nc.tensor.transpose(bank[k][:, P * t:P * (t + 1)], h[p][:, t, P * k:P * (k + 1)],
                                                   ident[:])
                    last.then_inc(h_turned, 1)
                pe.wait_ge(hT_ready, KD * b + KD)
                if not (isinstance(b, int) and b < 2):
                    pe.wait_ge(rank_read, b - 1)
                for c in range(KD):
                    for k in range(KD):
                        last = mm(bank[2 + c][:], wT_s[:, k, P * c:P * (c + 1)], hT[:, k, :],
                                  start=(k == 0), stop=(k == KD - 1))
                    last.then_inc(kt_mm, 1)
                for t in range(NT):
                    if t % 2 == 0:
                        pe.wait_ge(KT_ready, KD * b + t // 2 + 1)
                    for k in range(KD):
                        last = mm(bank[2 + t // 2][:, D * (t % 2):D * (t % 2 + 1)], hT[:, k, P * t:P * (t + 1)],
                                  wT_s[:, k, D:2 * D], start=(k == 0), stop=(k == KD - 1))
                    if t % 2 == 1:
                        last.then_inc(v_mm, 1)

            def share(b, c):
                if c == 0:
                    pe.wait_ge(V_ready, 2 * (b + 1) + 2 if not (isinstance(b, int) and b == B - 1) else 2 * B)
                else:
                    pe.wait_ge(share_hidden, KI * b + c)
                for n in range(2):
                    for k in range(KD):
                        last = mm(bank[2 + n][:], sgu_s[:, k, SI * n + P * c:SI * n + P * (c + 1)], h2T[:, k, :],
                                  start=(k == 0), stop=(k == KD - 1))
                        if c == 0 and n == 0 and k == 0:
                            pe.wait_ge(esigT_ready, b + 1)
                            apart(pe)
                            for t in range(NT):
                                turned = nc.tensor.transpose(bank[0][:, E * t:E * (t + 1)],
                                                             esigT[:, P * t:P * (t + 1)], ident[0:E, 0:E])
                            turned.then_inc(esig_turned, 1)
                last.then_inc(share_mm, 1)

            def share_out(b):
                pe.wait_ge(share_hidden, KI * b + KI)
                for t in range(NT):
                    for c in range(KI):
                        last = mm(bank[t // 2][:, D * (t % 2):D * (t % 2 + 1)], sh[:, c, P * t:P * (t + 1)],
                                  sdn_s[:, c, :], start=(c == 0), stop=(c == KI - 1))
                last.then_inc(share_down, 1)

            def rank_of(b):
                pe.wait_ge(share_hidden, KI * b + KI)
                pe.wait_ge(sel_ready, b + 1)
                flat = sel[:].rearrange("p t e -> p (t e)")
                mm(bank[2][:, 0:NT * E], earlier[:], flat, start=True, stop=False, skip_group_check=True)
                for t in range(1, NT):
                    mm(bank[2][:, E * t:E * NT], ones_bf[:], flat[:, 0:E * (NT - t)], start=False, stop=(t == NT - 1),
                       skip_group_check=True)
                for t in range(NT):
                    last = mm(bank[3][:, 0:E], ones_bf[:], sel[:, t, :], start=(t == 0), stop=(t == NT - 1))
                last.then_inc(rank_mm, 1)

            def score(b, i):
                keys = P * (i + 1)
                for k in range(KD):
                    mm(bank[4 + i % 2][:, 0:keys], hT[:, k, P * i:P * (i + 1)], KT[:, k, 0:keys],
                       start=(k == 0), stop=False)
                mm(bank[4 + i % 2][:, P * i:keys], ident_bf[:], causal[:], start=False, stop=True
                   ).then_inc(scored, 1)

            def attention(b, m, p, late, more):
                def turn(i):
                    pe.wait_ge(probs_ready, NT * b + i + 1)
                    for j in range(i + 1):
                        last = nc.tensor.transpose(turned_in(i)[:, P * j:P * (j + 1)], probs[i % 2][:, P * j:P * (j + 1)],
                                                   ident[:])
                    last.then_inc(probs_turned, 1)

                def attend(i):
                    pe.wait_ge(pT_ready, NT * b + i + 1)
                    if i == 0:
                        pe.wait_ge(V_ready, 2 * b + 2)
                    elif i < NT - 1:
                        pe.wait_ge(o_scaled, NT * b + i)
                    for j in range(i + 1):
                        last = mm(attended_in(i)[:, 0:D], pT_s[i % 2][:, P * j:P * (j + 1)], V[:, j, :], start=(j == 0),
                                  stop=(j == i))
                    last.then_inc(attended, 1)

                if not late:
                    score(b, 0)
                    score(b, 1)
                if late:
                    if isinstance(b, int) and b == 1 or not isinstance(b, int) or b:
                        pe.wait_ge(experts_loaded, 16 * (2 + KD))
                    share(b - 1, 0)
                turn(0)
                score(b, 2)
                attend(0)
                if late:
                    share(b - 1, 1)
                turn(1)
                score(b, 3)
                attend(1)
                if late:
                    rank_of(b - 1)
                    share_out(b - 1)
                turn(2)
                turn(3)
                attend(2)
                attend(3)
                if more:
                    front(b + 1, None, 1 - p)
                    score(b + 1, 0)
                    pe.wait_ge(o_scaled, NT * (b + 1))
                    score(b + 1, 1)
                pe.wait_ge(h2_ready, NT * b + NT)
                if late and not more:
                    pe.wait_ge(share_gated, b)
                for k in range(KD):
                    for t in range(NT):
                        last = nc.tensor.transpose(bank[k][:, P * t:P * (t + 1)], rows[p][:, t, P * k:P * (k + 1)],
                                                   ident[:])
                    last.then_inc(h2_turned, 1)
                pe.wait_ge(h2T_ready, KD * b + KD)
                for k in range(KD):
                    last = mm(bank[7][0:E, :], gateT_s[:, k, :], h2T[:, k, :], start=(k == 0), stop=(k == KD - 1))
                last.then_inc(logits_mm, 1)

            run_batches(pe, front, attention)
            pe.wait_ge(rank_read, B - 1)
            share(B - 1, 0)
            share(B - 1, 1)
            share_out(B - 1)
            rank_of(B - 1)
            pe.wait_ge(share_gated, B)
            pe.wait_ge(table_loaded, 16 * 3)
            pe.wait_ge(down_loaded, 16)

            expert_reg = [pe.alloc_register(f"expert{n}") for n in range(XG)]

            def load_expert(i, q, n, at):
                pe.reg_load(expert_reg[n], expert_row[0:1, bass.ds(i, 1)])

            def turn_rows(i, q, n, at):
                pe.wait_ge(xg_loaded[n], 16 * (q + 1))
                for k in range(KD):
                    last = nc.tensor.transpose(bank[n % 2][:, P * k:P * (k + 1)], xg[n][:, P * k:P * (k + 1)],
                                               ident[:])
                last.then_inc(xg_turned, 1)

            def up(i, q, n, at):
                e = pe.snap(expert_reg[n], min_val=0, max_val=E - 1)
                pe.wait_ge(xgT_ready, i + 1)
                for k in range(KD):
                    last = mm(bank[2 + n % 2][:, 0:2 * I], xgT[n % 2][:, P * k:P * (k + 1)],
                              gu_s[:, k, bass.ds(e, 1), :].rearrange("p a n -> p (a n)"), start=(k == 0),
                              stop=(k == KD - 1))
                last.then_inc(gu_mm, 1)

            def turn_hidden(i, q, n, at):
                pe.wait_ge(hs_ready, i + 1)
                nc.tensor.transpose(bank[4 + n % 2][:, 0:P], hs[n % 2], ident[:]).then_inc(hs_turned, 1)

            def down(i, q, n, at):
                e = pe.snap(expert_reg[n], min_val=0, max_val=E - 1)
                pe.wait_ge(hsT_ready, i + 1)
                if not (isinstance(i, int) and i < 2):
                    pe.wait_ge(y_ready, i - 1)
                mm(bank[6 + n % 2][:, 0:D], hsT[n % 2], dn_s[:, bass.ds(e, 1), :].rearrange("p a n -> p (a n)"),
                   start=True, stop=True).then_inc(y_mm, 1)

            run_blocks(pe, [turn_rows, up, load_expert, turn_hidden, down], [0, 1, 0, 2, 3],
                       later=lambda: pe.wait_ge(table_loaded, 16 * 3 * 2))

        @block.scalar
        def _(act):
            a = nc.scalar.activation
            copy = nc.scalar.copy
            act.wait_ge(c_loaded, 16)
            a(sig_c[:], cT_s[:], ACT.Exp, scale=-1.0).then_inc(exp_c_ready, 1)

            def normal(b, slot, scaled, ready):
                for t in range(NT):
                    act.wait_ge(scaled, NT * b + t + 1)
                    a(u[t], u[t], ACT.Copy, scale=rs_y[:, slot + t:slot + t + 1]).then_inc(ready, 1)

            def front(b, m, p):
                for k in range(KD):
                    act.wait_ge(h_turned, KD * b + k + 1)
                    copy(hT[:, k, :], bank[k][:]).then_inc(hT_ready, 1)
                for c in range(KD):
                    act.wait_ge(kt_mm, KD * b + c + 1)
                    copy(KT[:, c, :], bank[2 + c][:]).then_inc(KT_ready, 1)
                if not (isinstance(b, int) and b == 0):
                    normal(b - 1, 0, norm2_scaled, norm2_normal)
                for c in range(2):
                    act.wait_ge(v_mm, 2 * b + c + 1)
                    copy(V[:, 2 * c:2 * c + 2, :].rearrange("p a d -> p (a d)"), bank[2 + c][:]).then_inc(V_ready, 1)

            def share(b, c):
                act.wait_ge(share_mm, KI * b + c + 1)
                a(th[:], bank[2][:], ACT.Tanh, scale=0.5).then_inc(tanh_ready, 1)

            def attention(b, m, p, late, more):
                def exps(i):
                    keys = P * (i + 1)
                    act.wait_ge(max_ready, NT * b + i + 1)
                    if i >= 2:
                        act.wait_ge(probs_turned, NT * b + i - 1)
                    a(probs[i % 2][:, 0:keys], bank[4 + i % 2][:, 0:keys], ACT.Exp, bias=negmax[:, i:i + 1],
                      accum_out=rowsum[:, i:i + 1]).then_inc(probs_ready, 1)

                def copy_turned(i):
                    act.wait_ge(probs_turned, NT * b + i + 1)
                    if i >= 2:
                        act.wait_ge(attended, NT * b + i - 1)
                    copy(pT_s[i % 2][:, 0:P * (i + 1)], turned_in(i)[:, 0:P * (i + 1)]).then_inc(pT_ready, 1)

                exps(0)
                exps(1)
                if late:
                    share(b - 1, 0)
                copy_turned(0)
                exps(2)
                if late:
                    share(b - 1, 1)
                copy_turned(1)
                exps(3)
                if more:
                    normal(b + 1, NT, front_scaled, front_normal)
                copy_turned(2)
                copy_turned(3)
                if more:
                    front(b + 1, None, 1 - p)
                else:
                    normal(b, 0, norm2_scaled, norm2_normal)
                for k in range(KD):
                    act.wait_ge(h2_turned, KD * b + k + 1)
                    copy(h2T[:, k, :], bank[k][:]).then_inc(h2T_ready, 1)
                act.wait_ge(logits_mm, b + 1)
                a(esigT, bank[7][0:E, :], ACT.Exp, scale=-1.0).then_inc(esigT_ready, 1)

            normal(0, 0, front_scaled, front_normal)
            run_batches(act, front, attention)
            share(B - 1, 0)
            share(B - 1, 1)
            def copy_rows(i, q, n, at):
                act.wait_ge(xg_turned, i + 1)
                if not (isinstance(i, int) and i < 2):
                    act.wait_ge(gu_mm, i - 1)
                copy(xgT[n % 2], bank[n % 2][:, 0:D]).then_inc(xgT_ready, 1)

            def silu(i, q, n, at):
                act.wait_ge(gu_mm, i + 1)
                if not (isinstance(i, int) and i < 2):
                    act.wait_ge(hs_ready, i - 1)
                a(sg[n % 2], bank[2 + n % 2][:, 0:I], ACT.Silu).then_inc(silu_ready, 1)

            def copy_hidden(i, q, n, at):
                act.wait_ge(hs_turned, i + 1)
                if not (isinstance(i, int) and i < 2):
                    act.wait_ge(y_mm, i - 1)
                copy(hsT[n % 2], bank[4 + n % 2][:, 0:P]).then_inc(hsT_ready, 1)

            run_blocks(act, [copy_rows, silu, copy_hidden], [0, 1, 2])

            def store(n, m, k):
                act.wait_ge(out_ready, n + 1)
                apart(act)
                store_tile(act, n)
            run_tiles(act, [store])

        @block.vector
        def _(dve):
            v = nc.vector
            dve.wait_ge(exp_c_ready, 1)
            link = chain(dve, silu_c_steps, 0)
            link(v.tensor_scalar(sig_c[:], sig_c[:], 1.0, None, ALU.add))
            link(v.reciprocal(sig_c[:], sig_c[:]))
            v.tensor_tensor(silu_c[:], sig_c[:], cT_s[:], ALU.mult).then_inc(silu_c_steps, 1)
            dve.wait_ge(consts_ready, 1)

            STAT_STEPS = 5 + 3 * NEWTON

            def statistics(k, elements):
                n = NT * len(elements)
                link = chain(dve, stat_steps, STAT_STEPS * k)
                for t in range(NT):
                    last = v.bn_stats(st[:, t, :], tile_of(xs, elements[0], t))
                link(last)
                apart(dve)
                if len(elements) > 1:
                    dve.wait_ge(sums_ahead, k + 1)
                    apart(dve)
                for t in range(n):
                    last = v.bn_aggr(mv[:, t, :], st[:, t, :])
                link(last)
                y, var = rs_y[:, 0:n], rs_v[:, 0:n]
                link(v.tensor_scalar(var, mv[:, 0:n, 1], LN_EPS, None, ALU.add))
                link(v.tensor_scalar(rs_i[:, 0:n], var.bitcast(I32), 1, None, ALU.logical_shift_right))
                link(v.tensor_scalar(y.bitcast(I32), rs_i[:, 0:n], -1.0, float(RSQRT_SEED), ALU.mult, ALU.add))
                for step in range(NEWTON):
                    link(v.tensor_tensor(rs_a[:, 0:n], y, y, ALU.mult))
                    link(v.scalar_tensor_tensor(out=rs_b[:, 0:n], in0=rs_a[:, 0:n], scalar=-0.5, in1=var,
                                                op0=ALU.mult, op1=ALU.mult))
                    link(v.scalar_tensor_tensor(out=y, in0=rs_b[:, 0:n], scalar=1.5, in1=y,
                                                op0=ALU.add, op1=ALU.mult))
                assert link.done[0] == STAT_STEPS, link.done

            def sum_ahead(b):
                for t in range(NT):
                    last = v.bn_stats(st[:, NT + t, :], tile_of(xs, b, t))
                last.then_inc(sums_ahead, 1)

            def scale_tiles(b, slot, scale, scaled):
                for t in range(NT):
                    v.scalar_tensor_tensor(out=u[t], in0=tile_of(xs, b, t), scalar=mv[:, slot + t, 0:1], in1=scale,
                                           op0=ALU.subtract, op1=ALU.mult).then_inc(scaled, 1)

            def rest_of_modulation():
                dve.wait_ge(mod_mm, NM // 512)
                v.tensor_copy(mod[:, D * GA:D * (SB + 1)], mod_bank[1][0:B, :])
                v.tensor_scalar(mod[:, D * CB:D * GB], mod_bank[2][0:B, 0:D], 1.0, None, ALU.add)
                v.tensor_copy(mod[:, D * GB:D * (GB + 1)], mod_bank[2][0:B, D:2 * D]).then_inc(mod_steps, 1)
                dve.wait_ge(mod_steps, 1)
                gates = [(sign[:, j, :], mod[:, D * n:D * (n + 1)]) for j, n in enumerate((GA, GB))]
                for twice, gate in gates:
                    last = v.tensor_scalar(twice, gate, 0.0, 2.0, ALU.is_ge, ALU.mult)
                last.then_inc(mod_steps, 1)
                dve.wait_ge(mod_steps, 2)
                for twice, gate in gates:
                    last = v.scalar_tensor_tensor(out=gate, in0=twice, scalar=1.0, in1=gate, op0=ALU.subtract, op1=ALU.mult)
                last.then_inc(mod_steps, 1)
                dve.wait_ge(mod_steps, 3)
                for twice, gate in gates:
                    last = v.tensor_scalar(gate, gate, MIN_GATE, None, ALU.max)
                last.then_inc(mod_steps, 1)
                dve.wait_ge(mod_steps, 4)
                for twice, gate in gates:
                    last = v.scalar_tensor_tensor(out=gate, in0=twice, scalar=1.0, in1=gate, op0=ALU.subtract, op1=ALU.mult)
                last.then_inc(mod_ready, 1)

            def front(b, m, p):
                if isinstance(b, int) and b < 2:
                    dve.wait_ge(bc_first[p], 16)
                else:
                    dve.wait_ge(bc_loaded[p], 16 * (m + 1))
                apart(dve)
                if not (isinstance(b, int) and b < 2):
                    dve.wait_ge(h2_ready, NT * (b - 1))
                elif b == 1:
                    dve.wait_ge(h_ready, NT)
                scale_tiles(b, first_slot(b), bc[p][:, CA, :], front_scaled)
                if isinstance(b, int) and b == 0:
                    rest_of_modulation()

            CHOOSE = 13

            def choose_groups(b, between=None):
                link = chain(dve, choose_steps, CHOOSE * b)
                dve.wait_ge(esig_turned, b + 1)
                link(v.tensor_scalar(esig[:].rearrange("p t e -> p (t e)"), bank[0][:, 0:NT * E], 1.0, None, ALU.add))
                link(v.reciprocal(scores[:], esig[:]))
                link(v.tensor_tensor(sfc[:], scores[:], bias_s[:].to_broadcast([P, NT, E]), ALU.add))
                if between:
                    between()
                link(v.tensor_reduce(gs[:], sfc[:].rearrange("p t (g e) -> p t g e", e=EG), AX.X, ALU.max))
                pairs = [P, NT, N_GROUP, N_GROUP]
                other = gs[:].rearrange("p t (a o) -> p t a o", a=1).to_broadcast(pairs)
                this = gs[:].rearrange("p t (g a) -> p t g a", a=1).to_broadcast(pairs)
                v.tensor_tensor(cgt, other, this, ALU.is_gt)
                link(v.tensor_tensor(ceq, other, this, ALU.is_equal))
                link(v.tensor_tensor(ceq, ceq, before[:].rearrange("p (a g) o -> p a g o", a=1).to_broadcast(pairs),
                                     ALU.mult))
                link(v.tensor_tensor(cgt, cgt, ceq, ALU.add))
                link(v.tensor_reduce(rank[:], cgt, AX.X, ALU.add))
                link(v.tensor_scalar(rank[:], rank[:], float(TOPK_GROUP), None, ALU.is_lt))
                link(v.tensor_tensor(masked[:].rearrange("p t (g e) -> p (t g) e", e=EG),
                                     sfc[:].rearrange("p t (g e) -> p (t g) e", e=EG),
                                     rank[:].rearrange("p t (g a) -> p (t g) a", a=1)
                                     .to_broadcast([P, NT * N_GROUP, EG]), ALU.mult))
                return link

            def choose_experts(b, p, link):
                apart(dve)
                for t in range(NT):
                    last = v.max(m8[:, t, :], masked[:, t, :])
                link(last)
                apart(dve)
                for t in range(NT):
                    last = v.max_index(i8[:, t, :], m8[:, t, :], masked[:, t, :])
                link(last)
                link(v.tensor_copy(idx[:], i8[:, :, 0:TOP_K]))
                assert link.done[0] == CHOOSE, link.done
                each = [P, NT, TOP_K, E]
                v.tensor_tensor(eq[:], idx[:].rearrange("p t (j a) -> p t j a", a=1).to_broadcast(each),
                                experts_iota[:].rearrange("p (a b e) -> p a b e", a=1, b=1).to_broadcast(each),
                                ALU.is_equal).then_inc(eq_ready, 1)
                dve.wait_ge(eq_ready, b + 1)
                with nc.allow_low_precision(reason="at most one summand is not 0"):
                    v.tensor_reduce(sel[:], eq[:].rearrange("p t j e -> p t e j"), AX.X, ALU.add
                                    ).then_inc(sel_ready, 1)
                v.tensor_copy(rows[p][:, :, D:D + TOP_K], idx[:])
                v.tensor_copy(rows[p][:, :, D + TOP_K:D + 2 * TOP_K], dest0[:])

            PLACE = 6

            def read_ranks(b):
                dve.wait_ge(rank_mm, b + 1)
                for t in range(NT):
                    last = v.tensor_tensor(sfc[:, t, :], bank[2][:, E * t:E * (t + 1)], base[:], ALU.add)
                last.then_inc(rank_steps, 1)
                dve.wait_ge(rank_steps, b + 1)
                v.tensor_tensor(base[:], base[:], bank[3][:, 0:E], ALU.add).then_inc(rank_read, 1)

            def place(b, p):
                link = chain(dve, place_steps, PLACE * b)

                def of_each(table, out):
                    link(v.tensor_tensor(pr[:], eq[:], table[:].rearrange("p t (a e) -> p t a e", a=1)
                                         .to_broadcast([P, NT, TOP_K, E]), ALU.mult))
                    with nc.allow_low_precision(reason="at most one summand is not 0"):
                        return v.tensor_reduce(out, pr[:], AX.X, ALU.add)
                link(of_each(scores, raw[:]))
                link(v.tensor_reduce(tsum[:], raw[:], AX.X, ALU.add))
                link(v.tensor_scalar(tsum[:], tsum[:], 1e-20, None, ALU.add))
                link(v.reciprocal(tsum[:], tsum[:]))
                for t in range(NT):
                    v.tensor_scalar(rows[p][:, t, D + 2 * TOP_K:ROW], raw[:, t, :], tsum[:, t:t + 1], ROUTE_SCALE,
                                    ALU.mult, ALU.mult)
                v.tensor_scalar(dest0[:], dest0[:], float(S * TOP_K), None, ALU.add)
                of_each(sfc, pos[p][:]).then_inc(pos_ready, 1)
                assert link.done[0] == PLACE, link.done

            def share(b, c):
                dve.wait_ge(tanh_ready, KI * b + c + 1)
                if c == 0 and not (isinstance(b, int) and b == 0):
                    dve.wait_ge(share_added, b)
                    apart(dve)
                v.scalar_tensor_tensor(out=th[:], in0=th[:], scalar=1.0, in1=bank[2][:], op0=ALU.add, op1=ALU.mult
                                       ).then_inc(share_steps, 1)
                dve.wait_ge(share_steps, KI * b + c + 1)
                v.scalar_tensor_tensor(out=sh[:, c, :], in0=th[:], scalar=0.5, in1=bank[3][:], op0=ALU.mult,
                                       op1=ALU.mult).then_inc(share_hidden, 1)

            def gate_share(b):
                dve.wait_ge(share_down, b + 1)
                gb = tile_of(gb_all, 0, b).rearrange("p (a d) -> p a d", a=1).to_broadcast([P, 2, D])
                halves = [sh[:, c, :].rearrange("p (a d) -> p a d", a=2) for c in range(NT // 2)]
                for c in range(NT // 2):
                    last = v.tensor_tensor(halves[c], bank[c][:].rearrange("p (a d) -> p a d", a=2), gb, ALU.mult)
                last.then_inc(share_gated, 1)

            def attention(b, m, p, late, more):
                def row_max(b, i):
                    dve.wait_ge(scored, NT * b + i + 1)
                    v.tensor_reduce(negmax[:, i:i + 1], bank[4 + i % 2][:, 0:P * (i + 1)], AX.X, ALU.max, negate=True
                                    ).then_inc(max_ready, 1)

                steps = chain(dve, attend_steps, 2 * NT * b)

                def output(i):
                    dve.wait_ge(attended, NT * b + i + 1)
                    steps(v.reciprocal(rinv[:, i:i + 1], rowsum[:, i:i + 1]))
                    v.scalar_tensor_tensor(out=t1, in0=attended_in(i)[:, 0:D], scalar=rinv[:, i:i + 1], in1=h[p][:, i, :],
                                           op0=ALU.mult, op1=ALU.add).then_inc(o_scaled, 1)
                    dve.wait_ge(o_scaled, NT * b + i + 1)
                    steps(v.tensor_tensor(t2[i % 2], t1, bc[p][:, GA, :], ALU.mult))
                    v.tensor_tensor(tile_of(xs, b, i), tile_of(xs, b, i), t2[i % 2], ALU.add).then_inc(x2_ready, 1)

                if late:
                    link = choose_groups(b - 1)
                    share(b - 1, 0)
                    choose_experts(b - 1, 1 - p, link)
                else:
                    row_max(b, 0)
                    row_max(b, 1)
                row_max(b, 2)
                if isinstance(b, int) and b == 0:
                    for q in (0, 1):
                        dve.wait_ge(bc_loaded[q], 16)
                        apart(dve)
                output(0)
                if late:
                    share(b - 1, 1)
                row_max(b, 3)
                output(1)
                if more:
                    front(b + 1, m + 1 if p == 1 else m, 1 - p)
                if late:
                    read_ranks(b - 1)
                if late:
                    gate_share(b - 1)
                output(2)
                if not (isinstance(b, int) and (b == 0 or b >= B - 2)):
                    sum_ahead(b + 2)
                output(3)
                if isinstance(b, int) and b == 0:
                    dve.wait_ge(gb_loaded, 16)
                    apart(dve)
                    dve.wait_ge(x_rest_loaded, 16 * (B - 2))
                    apart(dve)
                    sum_ahead(2)
                dve.wait_ge(x2_ready, NT * b + NT)
                apart(dve)
                dve.wait_ge(h_ready, NT * (b + 2) if more else NT * B)
                apart(dve)
                statistics(b + 1, [b] if isinstance(b, int) and b >= B - 2 else [b, b + 2])
                scale_tiles(b, 0, bc[p][:, CB, :], norm2_scaled)
                if more:
                    row_max(b + 1, 0)
                    row_max(b + 1, 1)
                if late:
                    place(b - 1, 1 - p)

            dve.wait_ge(mod_mm, 1)
            v.tensor_copy(mod[:, 0:D], mod_bank[0][0:B, 0:D])
            v.tensor_scalar(mod[:, D:2 * D], mod_bank[0][0:B, D:2 * D], 1.0, None, ALU.add).then_inc(mod_first_ready, 1)
            for q in (0, 1):
                dve.wait_ge(x_loaded[q], 16)
                apart(dve)
            sum_ahead(1)
            statistics(0, [0, 1])
            run_batches(dve, front, attention)

            table_link = chain(dve, table_steps, 0)

            def blocks_of_experts(rounding, out):
                table_link(v.tensor_tensor(rows_of[:], base[:], area[:], ALU.subtract))
                table_link(v.tensor_scalar(blocks_i[:], rows_of[:], float(rounding), None, ALU.add))
                table_link(v.tensor_scalar(blocks_i[:], blocks_i[:], P.bit_length() - 1, None,
                                           ALU.logical_shift_right))
                table_link(v.tensor_copy(out[:], blocks_i[:]))

            def running_sum(src, out):
                step, k = 1, 0
                while step < E:
                    dst = out if 2 * step >= E else running[k % 2][:]
                    v.tensor_copy(dst[:, 0:step], src[:, 0:step])
                    table_link(v.tensor_tensor(dst[:, step:E], src[:, step:E], src[:, 0:E - step], ALU.add))
                    src, step, k = dst, 2 * step, k + 1

            def look_up(piece, slots, idle, column):
                n = slots + idle
                table_link(v.tensor_scalar(hit[:, 0:slots], cum[:, 0:slots], block_no[:, piece:piece + 1], None,
                                           ALU.is_le))
                table_link(v.tensor_reduce(slot[:], hit[:, 0:slots], AX.X, ALU.add))
                for out, values in ((hit, expert_of), (hit_first, first)):
                    last = v.scalar_tensor_tensor(out=out[:, 0:n], in0=slot_no[:, 0:n], scalar=slot[:, 0:1],
                                                  in1=values[:, 0:n], op0=ALU.is_equal, op1=ALU.mult)
                table_link(last)
                v.tensor_reduce(expert_f[:], hit[:, 0:n], AX.X, ALU.add)
                table_link(v.tensor_reduce(row_f[:], hit_first[:, 0:n], AX.X, ALU.add))
                v.tensor_copy(table_e[:, column:column + 1], expert_f[:])
                v.tensor_copy(table_f[:, column:column + 1], expert_f[:])
                table_link(v.scalar_tensor_tensor(out=row_f[:], in0=block_no[:, piece:piece + 1], scalar=float(P),
                                                  in1=row_f[:], op0=ALU.mult, op1=ALU.add))
                table_link(v.tensor_scalar(table_r[:, column:column + 1], row_f[:], float(E * CAP), None, ALU.min))

            dve.wait_ge(rank_read, B - 1)
            blocks_of_experts(0, full)
            running_sum(full[:], cum[:, 0:E])
            table_link(v.tensor_tensor(cum_ex[:], cum[:, 0:E], full[:], ALU.subtract))
            table_link(v.scalar_tensor_tensor(out=first[:, 0:E], in0=cum_ex[:], scalar=-float(P), in1=area[:],
                                              op0=ALU.mult, op1=ALU.add))
            for piece in range(NH):
                look_up(piece, E, 0, piece)
            dve.sem_inc(table_ready, 1)

            link = choose_groups(B - 1, lambda: share(B - 1, 0))
            share(B - 1, 1)
            choose_experts(B - 1, (B - 1) % 2, link)
            read_ranks(B - 1)
            dve.wait_ge(rank_read, B)
            v.tensor_copy(base_i[:], base[:]).then_inc(base_ready, 1)
            gate_share(B - 1)
            place(B - 1, (B - 1) % 2)

            blocks_of_experts(P - 1, blocks_f)
            table_link(v.tensor_tensor(rest[:], blocks_f[:], full[:], ALU.subtract))
            running_sum(rest[:], cum[:, E:2 * E])
            table_link(v.tensor_tensor(cum_ex[:], cum[:, E:2 * E], rest[:], ALU.subtract))
            table_link(v.tensor_scalar(cum[:, E:2 * E], cum[:, E:2 * E], cum[:, E - 1:E], None, ALU.add))
            table_link(v.tensor_scalar(cum_ex[:], cum_ex[:], cum[:, E - 1:E], None, ALU.add))
            table_link(v.scalar_tensor_tensor(out=first[:, E:2 * E], in0=cum_ex[:], scalar=-float(P), in1=area[:],
                                              op0=ALU.mult, op1=ALU.add))
            table_link(v.scalar_tensor_tensor(out=first[:, E:2 * E], in0=full[:], scalar=float(P),
                                              in1=first[:, E:2 * E], op0=ALU.mult, op1=ALU.add))
            look_up(NH - 1, 2 * E, 1, NH)
            dve.sem_inc(table_ready, 1)
            dve.wait_ge(share_added, B)
            dve.wait_ge(table_loaded, 16 * 3)

            def find_dest(i, q, n, at):
                dve.wait_ge(xg_loaded[n], 16 * (q + 1))
                apart(dve)
                v.scalar_tensor_tensor(out=match[:, n % 2],
                                       in0=xg[n][:, D:D + TOP_K].rearrange("p (a j) -> p a j", a=1)
                                       .to_broadcast([P, 2, TOP_K]), scalar=expert_bc[:, bass.ds(i, 1)],
                                       in1=xg[n][:, D + TOP_K:ROW].rearrange("p (a j) -> p a j", a=2),
                                       op0=ALU.is_equal, op1=ALU.mult).then_inc(dest_steps, 1)
                dve.wait_ge(dest_steps, 2 * i + 1)
                v.tensor_reduce(found[:, n, :], match[:, n % 2], AX.X, ALU.add).then_inc(dest_steps, 1)
                dve.wait_ge(dest_steps, 2 * i + 2)
                if not (isinstance(i, int) and i < XG):
                    dve.wait_ge(y_scattered[n], 16 * q)
                v.tensor_scalar(dest[n][:], found[:, n, 0:1], -1.0, None, ALU.add).then_inc(dest_ready, 1)

            def hidden(i, q, n, at):
                dve.wait_ge(silu_ready, i + 1)
                if not (isinstance(i, int) and i < 2):
                    dve.wait_ge(hs_turned, i - 1)
                v.tensor_tensor(hs[n % 2], sg[n % 2], bank[2 + n % 2][:, I:2 * I], ALU.mult).then_inc(hs_ready, 1)

            def copy_out(i, q, n, at):
                dve.wait_ge(y_mm, i + 1)
                v.tensor_scalar(yb[n], bank[6 + n % 2][:, 0:D], found[:, n, 1:2], None, ALU.mult
                                ).then_inc(y_ready, 1)

            run_blocks(dve, [find_dest, hidden, copy_out], [1, 1, 3],
                       later=lambda: dve.wait_ge(table_loaded, 16 * 3 * 2))

            def halve(n, m, k):
                dve.wait_ge(y_loaded[k], 16 * (m + 1))
                v.tensor_tensor(y3[k], yt[k][:, 0:3 * D], yt[k][:, 3 * D:6 * D], ALU.add).then_inc(halved, 1)

            def two_of_three(n, m, k):
                dve.wait_ge(halved, n + 1)
                v.tensor_tensor(y1[k], y3[k][:, 0:D], y3[k][:, D:2 * D], ALU.add).then_inc(added, 1)

            run_tiles(dve, [halve, two_of_three])


def kernel(**inputs):
    import numpy as np
    import concourse.bacc as bacc
    from concourse import mybir as mb
    from concourse.bass_utils import run_bass_kernel_spmd as run

    f = {k: np.asarray(a) for k, a in inputs.items()}
    arrays = {
        "x": f["L0_attn_x"], "wT": f["L0_attn_W"].T, "gateT": f["L0_ffn_gate_weight"].T,
        "bias": f["L0_ffn_e_score_correction_bias"],
        "guT": f["L0_ffn_experts_gate_up"].transpose(0, 2, 1), "dnT": f["L0_ffn_experts_down"].transpose(0, 2, 1),
        "sguT": np.concatenate([f["L0_ffn_shared_gate_w"], f["L0_ffn_shared_up_w"]], axis=0).T,
        "sdnT": f["L0_ffn_shared_down_w"].T,
        "cT": f["L0_c"].T, "wmod": f["L0_wmod"],
    }
    arrays = {k: np.ascontiguousarray(a) for k, a in arrays.items()}
    nc = bacc.Bacc("TRN2", target_bir_lowering=False, num_devices=1)
    args = [nc.dram_tensor(k, a.shape, mb.dt.from_np(a.dtype), kind="ExternalInput").ap() for k, a in arrays.items()]
    out = nc.dram_tensor("out", f["L0_attn_x"].shape, mb.dt.float32, kind="ExternalOutput").ap()
    build_adaln_block(nc, *args, out)
    r = run(nc, [arrays], core_ids=[0])
    return r.results[0]["out"]
```
